# Optimizing a Trainium2 kernel written in Bass

```python
import numpy as np
import jax
import jax.numpy as jnp

def _softmax(x, axis=-1):
    return jax.nn.softmax(x, axis=axis)

def _gelu(x):
    return jax.nn.gelu(x, approximate=True)

def _silu(x):
    return jax.nn.silu(x)

def _sigmoid(x):
    return jax.nn.sigmoid(x)

def _layernorm(x, axis=-1, eps=1e-05):
    m = jnp.mean(x, axis=axis, keepdims=True)
    v = jnp.var(x, axis=axis, keepdims=True)
    return (x - m) / jnp.sqrt(v + eps)

def _scatter_add(tgt, idx, src, axis=0):
    return tgt.at[idx].add(src)

def _segment_sum(src, seg, n):
    return jax.ops.segment_sum(src, seg, n)
kernel_name = 'mk_flamingo_gated_d1_seqx_r8_06ff4c'

def setup_inputs(seed: int=0):
    np.random.seed(seed)
    _w = jnp.asarray

    def _rec_inputs():
        import jax
        import jax.numpy as jnp
        _rk = jax.random.key(seed)
        x = -0.000929 + 1 * jax.random.normal(jax.random.fold_in(_rk, 1), (16, 128, 128), jnp.float32)
        _lenS = 128 - jax.random.randint(jax.random.fold_in(_rk, 7), (16,), 0, max(1, 128 // 4) + 1, jnp.int32)
        _lenS2 = 128 - jax.random.randint(jax.random.fold_in(_rk, 8), (16,), 0, max(1, 128 // 4) + 1, jnp.int32)
        _ctx_1024P = jax.random.normal(jax.random.fold_in(_rk, 11), (16, 16, 128), jnp.float32)
        _ctx_1024c = jax.random.dirichlet(jax.random.fold_in(_rk, 511), 0.3 * jnp.ones((16,), jnp.float32), (16, 128))
        _ctx_1024t = jnp.einsum('bsk,bkd->bsd', _ctx_1024c, _ctx_1024P)
        _ctx_1024t = _ctx_1024t * jax.lax.rsqrt(jnp.mean(jnp.square(_ctx_1024t)) + 1e-12) * 0.953939
        ctx_1024 = 0.000227908 + 0.99994 * (_ctx_1024t + 0.3 * jax.random.normal(jax.random.fold_in(_rk, 611), (16, 128, 128), jnp.float32))
        fside_BxSxS2_0 = jax.random.uniform(jax.random.fold_in(_rk, 12), (16, 128, 128), jnp.float32, 0.0, 0.999998)
        _validS = jnp.arange(128)[None, :] < _lenS[:, None]
        _validS2 = jnp.arange(128)[None, :] < _lenS2[:, None]
        _causal = jnp.tril(jnp.ones((128, 128), dtype=bool))
        mask_Bx1x1xS2_ff0 = jnp.where(jnp.ones((16, 1, 1, 128), dtype=bool), 0.0, -1000000000.0).astype(jnp.float32)
        _g = jax.random.normal(jax.random.fold_in(_rk, 9001), (2, 1), jnp.float32)
        _g = jnp.sign(_g) * jnp.maximum(jnp.abs(_g), 1.0) + (_g == 0) * 1.0
        g_xattn = _g[0]
        g_ffn = _g[1]
        return (x, ctx_1024, fside_BxSxS2_0, mask_Bx1x1xS2_ff0, g_xattn, g_ffn)
    x, ctx_1024, fside_BxSxS2_0, mask_Bx1x1xS2_ff0, g_xattn, g_ffn = _rec_inputs()

    def _L0_xattn_setup():
        import jax, jax.numpy as jnp
        import numpy as np
        B, F, T = (2, 64, 64)
        D, N, H = (128, 16, 64)
        K = 32
        FILT = 512
        L = 4
        EPS = 1e-06

        def _glorot(key, shape, fan_in, fan_out):
            lim = np.sqrt(6.0 / (fan_in + fan_out)).astype(np.float32)
            return jax.random.uniform(key, shape, jnp.float32, -lim, lim)

        def _norm(x):
            m = jnp.mean(x, axis=-1, keepdims=True)
            s = jnp.sqrt(jnp.mean((x - m) ** 2, axis=-1, keepdims=True))
            return (x - m) / (s + EPS)

        def _attention(x, src, dist, bias, Wq, Wk, Wv, Wo, Wth, bth, Wto, bto):
            q = jnp.einsum('bfd,dnh->bfnh', x, Wq) * H ** (-0.5)
            k = jnp.einsum('btd,dnh->btnh', src, Wk)
            v = jnp.einsum('btd,dnh->btnh', src, Wv)
            hbias = jax.nn.relu(dist[..., None] @ Wth + bth)
            qs_bias = (hbias @ Wto + bto)[..., 0]
            logits = jnp.einsum('btnh,bfnh->bnft', k, q)
            logits = logits + bias + qs_bias[:, None]
            w = jax.nn.softmax(logits, axis=-1)
            out = jnp.einsum('bnft,btnh->bfnh', w, v)
            return jnp.einsum('bfnh,nhd->bfd', out, Wo)
        key = jax.random.key(seed)
        ks = jax.random.split(key, 18)
        inp = {'decoder_inputs': jax.random.normal(ks[0], (B, F, D), jnp.float32), 'encoder_outputs': jax.random.normal(ks[1], (B, T, D), jnp.float32), 'decoder_times_dist': jax.random.uniform(ks[2], (B, F, F), jnp.float32), 'decoder_encoder_times_dist': jax.random.uniform(ks[3], (B, F, T), jnp.float32), 'dec_self_attn_bias': jnp.zeros((B, 1, 1, F), jnp.float32), 'enc_dec_attn_bias': jnp.zeros((B, 1, 1, T), jnp.float32), 'Wq': _glorot(ks[4], (L, D, N, H), D, D), 'Wk': _glorot(ks[5], (L, D, N, H), D, D), 'Wv': _glorot(ks[6], (L, D, N, H), D, D), 'Wo': _glorot(ks[7], (L, N, H, D), D, D), 'Wth': _glorot(ks[8], (L, 1, K), 1, K), 'bth': jnp.zeros((L, K), jnp.float32), 'Wto': _glorot(ks[9], (L, K, 1), K, 1), 'bto': jnp.zeros((L, 1), jnp.float32), 'Wf1': _glorot(ks[10], (L, D, FILT), D, FILT), 'bf1': jnp.zeros((L, FILT), jnp.float32), 'Wf2': _glorot(ks[11], (L, FILT, D), FILT, D), 'bf2': jnp.zeros((L, D), jnp.float32)}
        return inp
    _L0_xattn_all = _L0_xattn_setup()
    _L0_xattn_in = {k: v for k, v in _L0_xattn_all.items() if k in ('Wq', 'Wk', 'Wv', 'Wo', 'Wth', 'bth', 'Wto', 'bto', 'Wf1', 'bf1', 'Wf2', 'bf2')}
    del _L0_xattn_all

    def _L0_ffn_setup():
        import jax, jax.numpy as jnp
        import numpy as np
        NUM_HEADS = 16
        TOP_K = 2
        key = jax.random.key(seed)
        ks = jax.random.split(key, 5)
        B, S, D, E = (4, 256, 128, 8)
        scale = 0.02
        return {'x': jax.random.normal(ks[0], (B, S, D), dtype=jnp.float32), 'W_qkv': jax.random.normal(ks[1], (D, 3 * D), dtype=jnp.float32) * scale, 'b_qkv': jnp.zeros((3 * D,), dtype=jnp.float32), 'W_gate': jax.random.normal(ks[2], (D, E), dtype=jnp.float32) * scale, 'b_gate': jnp.zeros((E,), dtype=jnp.float32), 'W_experts': jax.random.normal(ks[3], (E, D, D), dtype=jnp.float32) * scale, 'b_experts': jnp.zeros((E, D), dtype=jnp.float32)}
    _L0_ffn_all = _L0_ffn_setup()
    _L0_ffn_in = {k: v for k, v in _L0_ffn_all.items() if k in ('W_qkv', 'b_qkv', 'W_gate', 'b_gate', 'W_experts', 'b_experts')}
    del _L0_ffn_all
    return {'x': x, 'ctx_1024': ctx_1024, 'fside_BxSxS2_0': fside_BxSxS2_0, 'mask_Bx1x1xS2_ff0': mask_Bx1x1xS2_ff0, 'g_xattn': g_xattn, 'g_ffn': g_ffn, 'L0_xattn_Wq': _L0_xattn_in['Wq'], 'L0_xattn_Wk': _L0_xattn_in['Wk'], 'L0_xattn_Wv': _L0_xattn_in['Wv'], 'L0_xattn_Wo': _L0_xattn_in['Wo'], 'L0_xattn_Wth': _L0_xattn_in['Wth'], 'L0_xattn_bth': _L0_xattn_in['bth'], 'L0_xattn_Wto': _L0_xattn_in['Wto'], 'L0_xattn_bto': _L0_xattn_in['bto'], 'L0_xattn_Wf1': _L0_xattn_in['Wf1'], 'L0_xattn_bf1': _L0_xattn_in['bf1'], 'L0_xattn_Wf2': _L0_xattn_in['Wf2'], 'L0_xattn_bf2': _L0_xattn_in['bf2'], 'L0_ffn_W_qkv': _L0_ffn_in['W_qkv'], 'L0_ffn_b_qkv': _L0_ffn_in['b_qkv'], 'L0_ffn_W_gate': _L0_ffn_in['W_gate'], 'L0_ffn_b_gate': _L0_ffn_in['b_gate'], 'L0_ffn_W_experts': _L0_ffn_in['W_experts'], 'L0_ffn_b_experts': _L0_ffn_in['b_experts']}

def reference(x, ctx_1024, fside_BxSxS2_0, mask_Bx1x1xS2_ff0, g_xattn, g_ffn, L0_xattn_Wq, L0_xattn_Wk, L0_xattn_Wv, L0_xattn_Wo, L0_xattn_Wth, L0_xattn_bth, L0_xattn_Wto, L0_xattn_bto, L0_xattn_Wf1, L0_xattn_bf1, L0_xattn_Wf2, L0_xattn_bf2, L0_ffn_W_qkv, L0_ffn_b_qkv, L0_ffn_W_gate, L0_ffn_b_gate, L0_ffn_W_experts, L0_ffn_b_experts):
    import jax
    import jax.numpy as jnp

    def _L0_xattn_ref(decoder_inputs, encoder_outputs, decoder_times_dist, decoder_encoder_times_dist, dec_self_attn_bias, enc_dec_attn_bias, Wq, Wk, Wv, Wo, Wth, bth, Wto, bto, Wf1, bf1, Wf2, bf2):
        import jax, jax.numpy as jnp
        import numpy as np
        B, F, T = (2, 64, 64)
        D, N, H = (128, 16, 64)
        K = 32
        FILT = 512
        L = 4
        EPS = 1e-06

        def _glorot(key, shape, fan_in, fan_out):
            lim = np.sqrt(6.0 / (fan_in + fan_out)).astype(np.float32)
            return jax.random.uniform(key, shape, jnp.float32, -lim, lim)

        def _norm(x):
            m = jnp.mean(x, axis=-1, keepdims=True)
            s = jnp.sqrt(jnp.mean((x - m) ** 2, axis=-1, keepdims=True))
            return (x - m) / (s + EPS)

        def _attention(x, src, dist, bias, Wq, Wk, Wv, Wo, Wth, bth, Wto, bto):
            q = jnp.einsum('bfd,dnh->bfnh', x, Wq) * H ** (-0.5)
            k = jnp.einsum('btd,dnh->btnh', src, Wk)
            v = jnp.einsum('btd,dnh->btnh', src, Wv)
            hbias = jax.nn.relu(dist[..., None] @ Wth + bth)
            qs_bias = (hbias @ Wto + bto)[..., 0]
            logits = jnp.einsum('btnh,bfnh->bnft', k, q)
            logits = logits + bias + qs_bias[:, None]
            w = jax.nn.softmax(logits, axis=-1)
            out = jnp.einsum('bnft,btnh->bfnh', w, v)
            return jnp.einsum('bfnh,nhd->bfd', out, Wo)
        x = decoder_inputs
        for i in range(L):
            y = _attention(_norm(x), encoder_outputs, decoder_encoder_times_dist, enc_dec_attn_bias, Wq[i], Wk[i], Wv[i], Wo[i], Wth[i], bth[i], Wto[i], bto[i])
            x = x + y
            y = jax.nn.relu(_norm(x) @ Wf1[i] + bf1[i]) @ Wf2[i] + bf2[i]
            x = x + y
        return _norm(x)

    def _L0_ffn_ref(x, W_qkv, b_qkv, W_gate, b_gate, W_experts, b_experts):
        import jax, jax.numpy as jnp
        import numpy as np
        NUM_HEADS = 16
        TOP_K = 2
        B, S, D = x.shape
        H = NUM_HEADS
        hd = D // H
        E = W_gate.shape[-1]
        qkv = (x @ W_qkv + b_qkv).reshape(B, S, 3, H, hd)
        q, k, v = (qkv[:, :, 0], qkv[:, :, 1], qkv[:, :, 2])
        attn = jnp.einsum('bqhd,bkhd->bhqk', q, k) / jnp.sqrt(jnp.asarray(hd, x.dtype))
        attn = jax.nn.softmax(attn, axis=-1)
        attn_out = jnp.einsum('bhqk,bkhd->bqhd', attn, v).reshape(B, S, D)
        gate = jax.nn.softmax(x @ W_gate + b_gate, axis=-1)
        top_g, top_i = jax.lax.top_k(gate, TOP_K)
        combine = jnp.sum(jax.nn.one_hot(top_i, E, dtype=x.dtype) * top_g[..., None], axis=2)
        expert_out = jnp.einsum('bsd,edf->bsef', x, W_experts) + b_experts
        moe_out = jnp.einsum('bsef,bse->bsf', expert_out, combine)
        return attn_out + moe_out
    x = x + jnp.tanh(g_xattn[0]) * _L0_xattn_ref(_layernorm(x, axis=-1), ctx_1024, fside_BxSxS2_0, fside_BxSxS2_0, mask_Bx1x1xS2_ff0, mask_Bx1x1xS2_ff0, L0_xattn_Wq, L0_xattn_Wk, L0_xattn_Wv, L0_xattn_Wo, L0_xattn_Wth, L0_xattn_bth, L0_xattn_Wto, L0_xattn_bto, L0_xattn_Wf1, L0_xattn_bf1, L0_xattn_Wf2, L0_xattn_bf2)
    x = x + jnp.tanh(g_ffn[0]) * _L0_ffn_ref(_layernorm(x, axis=-1), L0_ffn_W_qkv, L0_ffn_b_qkv, L0_ffn_W_gate, L0_ffn_b_gate, L0_ffn_W_experts, L0_ffn_b_experts)
    return x

_drawn_inputs = setup_inputs


def setup_inputs(seed=0):
    import zlib

    import numpy as np

    out = dict(_drawn_inputs(seed))
    spreads = {'L0_xattn_bth': (0.0, 0.8),
     'L0_xattn_bto': (0.0, 0.8),
     'L0_xattn_bf1': (0.0, 0.27),
     'L0_xattn_bf2': (0.0, 0.1),
     'L0_ffn_b_qkv': (0.0, 0.1),
     'L0_ffn_b_gate': (0.0, 0.452),
     'L0_ffn_b_experts': (0.0, 0.529)}
    factors = {'fside_BxSxS2_0': 8.0, 'L0_xattn_Wth': 8.0, 'L0_xattn_Wto': 8.0}
    for name, (base, spread) in spreads.items():
        noise = np.random.default_rng([zlib.crc32(name.encode()), seed]).standard_normal(out[name].shape)
        drawn = base * np.exp(spread * noise) if base else spread * noise
        out[name] = jnp.asarray(drawn.astype(out[name].dtype))
    for name, factor in factors.items():
        out[name] = (out[name] * factor).astype(out[name].dtype)
    return out
```

```python
from contextlib import ExitStack

import numpy as np
import concourse.bass as bass
from concourse import mybir

F32 = mybir.dt.float32
U32 = mybir.dt.uint32
ALU = mybir.AluOpType
ACT = mybir.ActivationFunctionType
AX_X = mybir.AxisListType.X

P = 128
BATCHES = 16
LAYERS = 4
HEADS = 16
HD = 64
BIAS_K = 32
FILT = 512
GROUP = 4
UNITS = LAYERS * BATCHES
GROUPS = UNITS // GROUP
GROUPS_PER_LAYER = BATCHES // GROUP
QUADS = 4
PAIRS = HEADS // 2
NORM_EPS = 1e-6
LN_EPS = 1e-5
BIG = 3.0e38

VEC_K = 24
POOL_K = BIAS_K - VEC_K
Z_SLOTS = 6
assert VEC_K % Z_SLOTS == 0


def plan(counts):
    ends = np.cumsum(np.array(counts).ravel()).reshape(np.shape(counts))
    return [[list(range(int(e) - n, int(e))) for n, e in zip(row, ends_)] for row, ends_ in zip(counts, ends)]


Z_PLAN = plan([[1, 2, 2, 1], [1, 2, 2, 1], [1, 2, 2, 1], [2, 2, 2, 0]])
TERM_PLAN = plan([[0, 2, 2, 1], [1, 2, 2, 1], [1, 2, 2, 1], [1, 2, 2, 2]])
assert Z_PLAN[-1][-2][-1] == TERM_PLAN[-1][-1][-1] == VEC_K - 1 and POOL_K == 2 * GROUP

C_WTH, C_BTH, C_WTO = 0, BIAS_K, 2 * BIAS_K
C_BTO = 3 * BIAS_K
C_PW, C_PB, C_HI, C_LO = [C_BTO + 1 + n * BIAS_K for n in range(4)]
C_ALL = C_BTO + 1 + 4 * BIAS_K

E_HEADS = 16
E_HD = 8
EXPERTS = 8
ROW_HEADS = 4
F_GROUPS = BATCHES // GROUP
VA = E_HD + 1


def wait(eng, sem, value):
    if isinstance(value, int) and value < 1:
        return
    eng.wait_ge(sem, value)


def wait_first(eng, consts, *counts):
    pairs = [(s, v) for s, v in zip(counts[::2], counts[1::2]) if not isinstance(v, int) or v > 0]
    pairs = [(s, v if isinstance(v, int) else eng.to_reg(v)) for s, v in pairs]
    eng.wait_ge(consts, 3)
    for s, v in pairs:
        eng.wait_ge(s, v)


def after(g, i, per, k=0):
    return g * (GROUP * per) + (i * per + k + 1)


def block_program(nc, x, ctx_in, dist, mask, g_xattn, g_ffn, Wq, Wk, Wv, Wo, Wth, bth, Wto, bto,
                  Wf1, bf1, Wf2, bf2, W_qkv, b_qkv, W_gate, b_gate, W_experts, b_experts, out):
    with ExitStack() as stack:
        def sb(name, shape, dt=F32):
            return stack.enter_context(nc.sbuf_tensor(name, shape, dt))

        def sem(name):
            return stack.enter_context(nc.semaphore(name))

        ident = sb("ident", [P, P])
        half = sb("half", [P, BATCHES])
        x_raw = sb("x_raw", [P, BATCHES, P])
        c_raw = sb("c_raw", [P, BATCHES, P])
        x_all = sb("x_all", [P, BATCHES, P])
        ctxT_all = sb("ctxT_all", [P, BATCHES, P])
        ln_st = sb("ln_st", [P, BATCHES, 6])
        ln_mv = sb("ln_mv", [P, BATCHES, 2])
        ln_ve = sb("ln_ve", [P, BATCHES])
        ln_sd = sb("ln_sd", [P, BATCHES])
        ln_rs = sb("ln_rs", [P, BATCHES])
        wq = sb("wq", [P, HEADS * HD])
        wk = sb("wk", [P, HEADS * HD])
        wv = sb("wv", [P, HEADS * HD])
        wo = sb("wo", [P, PAIRS, P])
        wf1 = sb("wf1", [P, FILT])
        wf2 = sb("wf2", [P, FILT // P, P])
        bf1c = sb("bf1c", [P, FILT // P])
        bf2b = sb("bf2b", [P, P])
        dist_g = sb("dist_g", [P, GROUP, P])
        mask_g = sb("mask_g", [P, GROUP, P])
        cst_all = sb("cst_all", [P, LAYERS, C_ALL])
        cst = sb("cst", [P, C_ALL])
        relu_z = sb("relu_z", [P, Z_SLOTS, GROUP * P])
        clamp_in = sb("clamp_in", [P, 2, GROUP * P])
        clamped = sb("clamped", [P, 2, GROUP * P])
        pool_acc = sb("pool_acc", [P, GROUP, P])
        bias_acc = sb("bias_acc", [P, GROUP * P])
        bias = sb("bias", [P, GROUP, P])
        xs = sb("xs", [P, GROUP, P])
        ctxT = sb("ctxT", [P, 2, P])
        h = sb("h", [P, 2, P])
        hT = sb("hT", [P, 2, P])
        h2 = sb("h2", [P, 2, P])
        h2T = sb("h2T", [P, 2, P])
        st = sb("st", [P, 2, 2, 6])
        mv = sb("mv", [P, 2, 2, 2])
        sd = sb("sd", [P, 2, 2])
        sde = sb("sde", [P, 2, 2])
        rs = sb("rs", [P, 2, 2])
        kT = sb("kT", [P, 2, PAIRS, P])
        qT = sb("qT", [P, 2, PAIRS, P])
        v = sb("v", [P, 2, HEADS * HD])
        score = sb("score", [P, QUADS, 4, P])
        nmax = sb("nmax", [P, QUADS, 4])
        prob = sb("prob", [P, QUADS, 4, P])
        rsum = sb("rsum", [P, QUADS, 4])
        rinv = sb("rinv", [P, QUADS, 4])
        probT = sb("probT", [P, QUADS, 4 * P])
        oT = sb("oT", [P, 2, PAIRS, P])
        hid = sb("hid", [P, 2, FILT // P, P])
        xb = sb("xb", [P, 2, P])
        gates_in = sb("gates_in", [P, 2])
        tg = sb("tg", [P, 2])
        wqk = sb("wqk", [P, 2 * P])
        wvg = sb("wvg", [P, P + EXPERTS])
        we = sb("we", [P, EXPERTS, P])
        be = sb("be", [EXPERTS, P])
        bqk = sb("bqk", [P, 2])
        bvg = sb("bvg", [P, P + EXPERTS])
        head_rows = sb("head_rows", [P, E_HEADS])
        head_mask = sb("head_mask", [P, ROW_HEADS])
        eidx = sb("eidx", [P, EXPERTS])
        xr = sb("xr", [P, GROUP, P])
        x4 = sb("x4", [P, GROUP, P])
        delta = sb("delta", [P, 2, P])
        x1 = sb("x1", [P, GROUP, P])
        hF = sb("hF", [P, 2, P])
        hFT = sb("hFT", [P, 2, P])
        qm = sb("qm", [P, 2, ROW_HEADS, P])
        kF = sb("kF", [P, 2, P])
        vF = sb("vF", [P, 2, E_HEADS, VA])
        stF = sb("stF", [P, 2, 2, 6])
        mvF = sb("mvF", [P, 2, 2, 2])
        tinyF = sb("tinyF", [P, 2, 8])
        gate = sb("gate", [P, 2, 5, EXPERTS])
        topi = sb("topi", [P, 2, EXPERTS], U32)
        gsum = sb("gsum", [P, 2, 2])
        nmaxF = sb("nmaxF", [P, QUADS, 4])
        rinvF = sb("rinvF", [P, E_HEADS])
        comb = sb("comb", [P, 2, P])
        combT = sb("combT", [EXPERTS, 2, P])
        accF = sb("accF", [P, P])
        outF = sb("outF", [P, 2, P])

        def bank(name):
            return stack.enter_context(nc.psum_tensor(name, [P, 512], F32))

        L = [bank("L0"), bank("L1")]
        T = [bank("T0"), bank("T1")]
        O = bank("O")
        M0, M1, M2 = bank("M0"), bank("M1"), bank("M2")

        consts = sem("consts")
        x_in, c_in = sem("x_in"), sem("c_in")
        ln_bn, ln_mvd, ln_vd, ln_sdd, ln_rd, ln_done = [sem("ln_" + n) for n in ("bn", "mvd", "vd", "sdd", "rd", "done")]
        cT_done, cT_kept = sem("cT_done"), sem("cT_kept")
        w_k, w_v, w_q, w_o, w_f1, w_f2, w_b1, w_b2 = [sem("w_" + n) for n in "k v q o f1 f2 b1 b2".split()]
        cst_in, cst_mul, cst_ready, dist_in, cv_in, cp_in = [sem(n) for n in ("cst_in", "cst_mul", "cst_ready", "dist_in", "cv_in", "cp_in")]
        z_done, term_done, bias_done = sem("z_done"), sem("term_done"), sem("bias_done")
        pool_mul, pool_clamp, pool_sum = sem("pool_mul"), sem("pool_clamp"), sem("pool_sum")
        xs_in = [sem(f"xs_in{i}") for i in range(GROUP)]
        xs_out = [sem(f"xs_out{i}") for i in range(GROUP)]
        ctx_slot = [sem(f"ctx_slot{i}") for i in range(2)]
        bn, var, sdev, sdeps, rstd, h_done = [[sem(f"{n}{a}") for a in "ab"] for n in ("bn", "var", "sdev", "sdeps", "rstd", "h_done")]
        hT_done, hT_kept, h2T_done, h2T_kept = sem("hT_done"), sem("hT_kept"), sem("h2T_done"), sem("h2T_kept")
        k_done, v_done, q_done = sem("k_done"), sem("v_done"), sem("q_done")
        k_kept = [sem(f"k_kept{i}") for i in range(2)]
        v_kept = [sem(f"v_kept{i}") for i in range(2)]
        q_kept = [sem(f"q_kept{i}") for i in range(2)]
        qk_done, scored, exp_done, inv_done, normed = [sem(n) for n in ("qk_done", "scored", "exp_done", "inv_done", "normed")]
        pT_done = sem("pT_done")
        pT_even, pT_odd = sem("pT_even"), sem("pT_odd")
        pv_done, o_kept, wo_done = sem("pv_done"), sem("o_kept"), sem("wo_done")
        resid1, resid2, xb_done = sem("resid1"), sem("resid2"), sem("xb_done")
        f1_done, hid_kept, f2_done = sem("f1_done"), sem("hid_kept"), sem("f2_done")
        f_consts, f_in, f_gate_in, tanh_done = sem("f_consts"), sem("f_in"), sem("f_gate_in"), sem("tanh_done")
        x4_in = [sem(f"x4_in{i}") for i in range(GROUP)]
        xr_in = [sem(f"xr_in{i}") for i in range(GROUP)]
        out_st = [sem(f"out_st{i}") for i in range(2)]
        fbn, fvar, fve, fsd, fsde, frs, frg = [[sem(f"f{n}{a}") for a in "ab"] for n in ("bn", "var", "ve", "sd", "sde", "rs", "rg")]
        fdelta, fx1, fh, fhT_done, fhT_kept = [sem("f_" + n) for n in ("delta", "x1", "h", "hT_done", "hT_kept")]
        fq_done, fk_done, fv_done, fq_kept, fk_kept, fv_kept, fg_kept = [sem("f_" + n) for n in ("q_done", "k_done", "v_done", "q_kept", "k_kept", "v_kept", "g_kept")]
        fqk, fmax, fexp, fT, fT_kept, fpv, fsums, fatt = [sem("f_" + n) for n in ("qk", "max", "exp", "T", "T_kept", "pv", "sums", "att")]
        fg_top, fg_neg, fg_exp, fg_inv, fg_soft, fg_top2, fg_idx, fg_idxf, fg_c0, fg_c1, fg_comb = [sem("f_g" + n) for n in ("top", "neg", "exp", "inv", "soft", "top2", "idx", "idxf", "c0", "c1", "comb")]
        fex_acc, f_prep = sem("f_ex_acc"), sem("f_prep")
        fcT, fcT_kept, fex, fbe, facc, fout = [sem("f_" + n) for n in ("cT", "cT_kept", "ex", "be", "acc", "out")]

        block = stack.enter_context(nc.Block())

        def walk(eng, step, groups=GROUPS, before=1, behind=2):
            for i in range(-before, GROUP):
                step(0, i)
            with eng.Fori(1, groups - 1) as g:
                for i in range(GROUP):
                    step(g, i)
            for i in range(GROUP + behind):
                step(groups - 1, i)

        def there(g, i):
            return not isinstance(g, int) or 0 <= GROUP * g + i < UNITS

        def f_there(g, i):
            return not isinstance(g, int) or 0 <= GROUP * g + i < BATCHES

        def layer_of(g, i):
            return (g + i // GROUP) >> 2

        @block.sync
        def _(sp):
            def load_cst(g, a, b, signal):
                sp.dma_start(cst[:, a:b], cst_all[:, bass.ds(g >> 2, 1), a:b].rearrange("p o c -> p (o c)")).then_inc(signal, 16)

            def load_dist(g):
                b = (g & 3) * GROUP
                sp.dma_start(dist_g[:, :, :], dist[bass.ds(b, GROUP), :, :].rearrange("b f t -> f b t")).then_inc(dist_in, 16)
                load_cst(g, C_WTH, C_WTO, dist_in)

            def load_wto(g):
                b = (g & 3) * GROUP
                load_cst(g, C_WTO, C_PW, cv_in)
                sp.dma_start(mask_g[:, :, :], mask[bass.ds(b, GROUP), 0, :, :].rearrange("b o t -> o b t").broadcast_to([P, GROUP, P])).then_inc(cv_in, 16)

            def load_k(l):
                sp.dma_start(wk[:, :], Wk[bass.ds(l, 1), :, :, :].rearrange("l d n h -> d (l n h)")).then_inc(w_k, 16)

            def load_vq(l):
                sp.dma_start(wv[:, :], Wv[bass.ds(l, 1), :, :, :].rearrange("l d n h -> d (l n h)")).then_inc(w_v, 16)

            def load_q(l):
                sp.dma_start(wq[:, :], Wq[bass.ds(l, 1), :, :, :].rearrange("l d n h -> d (l n h)")).then_inc(w_q, 16)

            def load_o(l):
                sp.dma_start(wo[:, :, :], Wo[bass.ds(l, 1), :, :, :].rearrange("l (j r) h d -> (r h) (l j) d", r=2)).then_inc(w_o, 16)

            def load_f1(l):
                sp.dma_start(wf1[:, :], Wf1[bass.ds(l, 1), :, :].rearrange("l d f -> d (l f)")).then_inc(w_f1, 16)

            def load_f2(l):
                sp.dma_start(wf2[:, :, :], Wf2[bass.ds(l, 1), :, :].rearrange("l (c p) d -> p (l c) d", p=P)).then_inc(w_f2, 16)

            def load_b1(l):
                sp.dma_start(bf1c[:, :], bf1[bass.ds(l, 1), :].rearrange("l (c p) -> p (l c)", p=P), allow_slow_non_contiguous=True).then_inc(w_b1, 16)

            def load_b2(l):
                sp.dma_start(bf2b[:, :], bf2[bass.ds(l, 1), :].broadcast_to([P, P])).then_inc(w_b2, 16)

            def load_x_slot(g, i):
                s = i % GROUP
                wait_first(sp, consts, xs_out[s], (g + (i // GROUP)) * 16)
                b = ((g + i // GROUP) & 3) * GROUP + s
                sp.dma_start(xs[:, s, :], x_all[:, bass.ds(b, 1), :].rearrange("p o d -> p (o d)")).then_inc(xs_in[s], 16)

            def load_ctx_slot(g, i):
                wait_first(sp, consts, v_done, after(g, i - 2, 2, 1))
                b = ((g + i // GROUP) & 3) * GROUP + i % GROUP
                sp.dma_start(ctxT[:, i % 2, :], ctxT_all[:, bass.ds(b, 1), :].rearrange("p o d -> p (o d)")).then_inc(ctx_slot[i % 2], 16)

            def store_x_slot(g, i):
                s = i % GROUP
                b = ((g + i // GROUP) & 3) * GROUP + s
                wait_first(sp, consts, resid2, after(g, i, 1))
                sp.dma_start(x_all[:, bass.ds(b, 1), :].rearrange("p o d -> p (o d)"), xs[:, s, :]).then_inc(xs_out[s], 16)

            for w, col in ((Wth.rearrange("l o k -> o l k"), C_WTH), (bth.rearrange("(o l) k -> o l k", o=1), C_BTH),
                           (Wto.rearrange("l k o -> o l k"), C_WTO)):
                sp.dma_start(cst_all[:, :, col:col + BIAS_K], w.broadcast_to([P, LAYERS, BIAS_K])).then_inc(cst_in, 16)
            sp.dma_start(cst_all[:, :, C_BTO:C_BTO + 1], bto.rearrange("(o l) k -> o l k", o=1).broadcast_to([P, LAYERS, 1]),
                         allow_slow_non_contiguous=True).then_inc(cst_in, 16)
            sp.dma_start(c_raw[:, :, :], ctx_in.rearrange("b t d -> t b d")).then_inc(c_in, 16)
            sp.dma_start(x_raw[:, :, :], x.rearrange("b s d -> s b d")).then_inc(x_in, 16)
            wait_first(sp, consts, cst_in, 64)
            load_dist(0)
            load_wto(0)
            wait_first(sp, consts, cst_ready, 4)
            load_cst(0, C_PW, C_ALL, cp_in)
            load_k(0)
            load_vq(0)
            load_q(0)
            load_o(0)
            load_f1(0)
            load_f2(0)
            load_b1(0)
            load_b2(0)
            sp.dma_start(gates_in[:, 0:1], g_xattn.rearrange("(o n) -> o n", o=1).broadcast_to([P, 1])).then_inc(f_gate_in, 16)
            sp.dma_start(gates_in[:, 1:2], g_ffn.rearrange("(o n) -> o n", o=1).broadcast_to([P, 1])).then_inc(f_gate_in, 16)
            sp.dma_start(wqk[:, :], W_qkv[:, 0:2 * P]).then_inc(f_in, 16)
            sp.dma_start(wvg[:, 0:P], W_qkv[:, 2 * P:3 * P]).then_inc(f_in, 16)
            sp.dma_start(wvg[:, P:P + EXPERTS], W_gate).then_inc(f_in, 16)
            sp.dma_start(we[:, :, :], W_experts.rearrange("e d f -> d e f")).then_inc(f_in, 16)
            sp.dma_start(be[:, :], b_experts).then_inc(f_in, 16)
            sp.dma_start(bqk[:, :], b_qkv[0:2 * P].rearrange("(a p) -> p a", p=P), allow_slow_non_contiguous=True).then_inc(f_in, 16)
            sp.dma_start(bvg[:, 0:P], b_qkv[2 * P:3 * P].rearrange("(o n) -> o n", o=1).broadcast_to([P, P])).then_inc(f_in, 16)
            sp.dma_start(bvg[:, P:P + EXPERTS], b_gate.rearrange("(o n) -> o n", o=1).broadcast_to([P, EXPERTS])).then_inc(f_in, 16)
            sp.wait_ge(cT_kept, 4)
            load_ctx_slot(0, 0)
            load_ctx_slot(0, 1)
            wait_first(sp, consts, ln_done, BATCHES)
            load_x_slot(0, 0)
            load_x_slot(0, 1)
            wait_first(sp, consts, z_done, VEC_K)
            wait_first(sp, consts, pool_clamp, POOL_K)
            load_dist(1)
            load_cst(1, C_PW, C_ALL, cp_in)
            sp.wait_ge(bias_done, 1)
            load_wto(1)

            def group(l, gg, first=False, last=False):
                g = l * GROUPS_PER_LAYER + gg
                for i in range(GROUP):
                    if there(g, i - 2):
                        store_x_slot(g, i - 2)
                    if there(g, i + 2):
                        load_x_slot(g, i + 2)
                        load_ctx_slot(g, i + 2)
                    if isinstance(gg, int) and gg == 0 and not first:
                        if i == 0:
                            wait_first(sp, consts, wo_done, after(g, -1, 1))
                            load_o(l)
                            wait_first(sp, consts, xb_done, after(g, -1, 1))
                            load_b2(l)
                        if i == 1:
                            wait_first(sp, consts, f1_done, after(g, -1, 1))
                            load_f1(l)
                            wait_first(sp, consts, hid_kept, after(g, -1, 1))
                            load_b1(l)
                            wait_first(sp, consts, f2_done, after(g, -1, 1))
                            load_f2(l)
                    if isinstance(gg, int) and gg == GROUPS_PER_LAYER - 1 and not last and i == 2:
                        wait_first(sp, consts, k_done, after(g, GROUP - 1, 2, 1))
                        load_k(l + 1)
                        wait_first(sp, consts, v_done, after(g, GROUP - 1, 2, 1))
                        load_vq(l + 1)
                        wait_first(sp, consts, q_done, after(g, GROUP - 1, 2, 1))
                        load_q(l + 1)
                if there(g, 2 * GROUP):
                    wait_first(sp, consts, z_done, (g + 2) * VEC_K, pool_clamp, (g + 2) * POOL_K)
                    load_dist(g + 2)
                    load_cst(g + 2, C_PW, C_ALL, cp_in)
                    wait_first(sp, consts, bias_done, g + 2)
                    load_wto(g + 2)

            for l in range(LAYERS):
                group(l, 0, first=l == 0)
                if l == LAYERS - 1:
                    group(l, 1)
                    group(l, 2)
                else:
                    with sp.Fori(1, GROUPS_PER_LAYER - 1) as gg:
                        group(l, gg)
                group(l, GROUPS_PER_LAYER - 1, last=l == LAYERS - 1)
            for i in range(GROUP, GROUP + 2):
                store_x_slot(GROUPS - 1, i - 2)

            def load_rows(g, i):
                s = i % GROUP
                b = (g + i // GROUP) * GROUP + s
                if isinstance(b, int):
                    sp.wait_ge(xs_out[s], GROUPS * 16)
                wait_first(sp, consts, fx1, after(g, i - GROUP, 1))
                sp.dma_start(x4[:, s, :], x_all[:, bass.ds(b, 1), :].rearrange("p o d -> p (o d)")).then_inc(x4_in[s], 16)
                sp.dma_start(xr[:, s, :], x[bass.ds(b, 1), :, :].rearrange("o s d -> (o s) d")).then_inc(xr_in[s], 16)

            def store_rows(g, i):
                wait_first(sp, consts, fout, after(g, i, 1))
                b = (g + i // GROUP) * GROUP + i % GROUP
                sp.dma_start(out[bass.ds(b, 1), :, :].rearrange("o s d -> (o s) d"), outF[:, i % 2, :]).then_inc(out_st[i % 2], 16)

            def f_step(g, i):
                if f_there(g, i - 1):
                    store_rows(g, i - 1)
                if f_there(g, i + 3):
                    load_rows(g, i + 3)

            walk(sp, f_step, F_GROUPS, 3, 1)
            for a in range(2):
                sp.wait_ge(out_st[a], BATCHES // 2 * 16)

        @block.tensor
        def _(pe):
            mm = nc.tensor.matmul

            pe.wait_ge(consts, 3)
            pe.wait_ge(c_in, 16)
            for n in range(BATCHES // 4):
                wait(pe, cT_kept, n - 1)
                for m in range(4):
                    last = nc.tensor.transpose(T[n % 2][:, m * P:(m + 1) * P], c_raw[:, 4 * n + m, :], ident[:, :])
                last.then_inc(cT_done, 1)
            pe.wait_ge(cT_kept, 4)

            def scores(g, i, octet):
                s = i % 2
                if octet == 0:
                    for a in range(2):
                        pe.wait_ge(k_kept[a], after(g, i, 1))
                        pe.wait_ge(q_kept[a], after(g, i, 1))
                wait(pe, scored, after(g, i, 4, 2 * octet - 1))
                for m in range(4):
                    for r in range(2):
                        j = 4 * octet + m
                        last = mm(L[r][:, m * P:(m + 1) * P], qT[64 * r:64 * r + 64, s, j, :], kT[64 * r:64 * r + 64, s, j, :],
                                  start=True, stop=True)
                        if m == 3:
                            last.then_inc(qk_done, 1)

            def turn(g, i, c):
                pe.wait_ge(normed, after(g, i, 4, c))
                wait(pe, pT_odd if c % 2 else pT_even, after(g, i, 2, c // 2 - 1))
                for m in range(4):
                    last = nc.tensor.transpose(T[c % 2][:, m * P:(m + 1) * P], prob[:, c, m, :], ident[:, :])
                last.then_inc(pT_done, 1)

            def apply(g, i, octet):
                if octet == 0:
                    for a in range(2):
                        pe.wait_ge(v_kept[a], after(g, i, 1))
                pe.wait_ge(pT_even, after(g, i, 2, octet))
                pe.wait_ge(pT_odd, after(g, i, 2, octet))
                wait(pe, o_kept, after(g, i, 2, octet - 1))
                for m in range(4):
                    for r in range(2):
                        n = 8 * octet + 2 * m + r
                        last = mm(O[64 * r:64 * r + 64, m * P:(m + 1) * P], v[:, i % 2, n * HD:(n + 1) * HD],
                                  probT[:, 2 * octet + r, m * P:(m + 1) * P], start=True, stop=True)
                last.then_inc(pv_done, 1)

            def project(dst, w, src, half_):
                for m in range(4):
                    j = 4 * half_ + m
                    last = mm(dst[:, m * P:(m + 1) * P], w[:, j * P:(j + 1) * P], src, start=True, stop=True)
                return last

            def keys(g, i, a):
                if a == 0:
                    pe.wait_ge(ctx_slot[i % 2], (g * 2 + i // 2 + 1) * 16)
                    if i % GROUP == 0:
                        pe.wait_ge(w_k, layer_of(g, i) * 16 + 16)
                    wait(pe, q_kept[0], after(g, i - 1, 1))
                else:
                    pe.wait_ge(k_kept[0], after(g, i, 1))
                project(M0, wk, ctxT[:, i % 2, :], a).then_inc(k_done, 1)

            def values(g, i, a):
                if a == 0:
                    if i % GROUP == 0:
                        pe.wait_ge(w_v, layer_of(g, i) * 16 + 16)
                    wait(pe, hid_kept, after(g, i - 3, 1))
                    wait(pe, q_kept[1], after(g, i - 1, 1))
                else:
                    pe.wait_ge(k_kept[1], after(g, i, 1))
                mm((M0 if a else M1)[:, :], ctxT[:, i % 2, :], wv[:, a * 512:(a + 1) * 512], start=True, stop=True).then_inc(v_done, 1)

            def queries(g, i, a):
                if a == 0:
                    pe.wait_ge(hT_kept, after(g, i, 1))
                    if i % GROUP == 0:
                        pe.wait_ge(w_q, layer_of(g, i) * 16 + 16)
                    pe.wait_ge(v_kept[1], after(g, i, 1))
                else:
                    pe.wait_ge(v_kept[0], after(g, i, 1))
                project(M1 if a else M0, wq, hT[:, i % 2, :], a).then_inc(q_done, 1)

            def step(g, i):
                nxt, cur, prev, old = there(g, i + 1), there(g, i), there(g, i - 1), there(g, i - 2)
                if prev:
                    turn(g, i - 1, 2)
                if nxt:
                    keys(g, i + 1, 0)
                if old:
                    pe.wait_ge(h_done[1], after(g, i - 2, 1))
                    wait(pe, resid1, after(g, i - 2, 1))
                    nc.tensor.transpose(M2[:, 0:P], h2[:, i % 2, :], ident[:, :]).then_inc(h2T_done, 1)
                if cur:
                    scores(g, i, 0)
                if old:
                    pe.wait_ge(h2T_kept, after(g, i - 2, 1))
                    if i % GROUP == 2:
                        pe.wait_ge(w_f1, layer_of(g, i - 2) * 16 + 16)
                    if cur:
                        wait(pe, q_kept[1], after(g, i, 1))
                    else:
                        pe.wait_ge(hid_kept, after(g, i - 3, 1))
                    for c in range(FILT // P):
                        last = mm(M1[:, c * P:(c + 1) * P], wf1[:, c * P:(c + 1) * P], h2T[:, i % 2, :], start=True, stop=True)
                    last.then_inc(f1_done, 1)
                if prev:
                    turn(g, i - 1, 3)
                if nxt:
                    pe.wait_ge(h_done[0], after(g, i + 1, 1))
                    wait(pe, h2T_kept, after(g, i - 2, 1))
                    nc.tensor.transpose(M2[:, 0:P], h[:, (i + 1) % 2, :], ident[:, :]).then_inc(hT_done, 1)
                    keys(g, i + 1, 1)
                    values(g, i + 1, 0)
                if prev:
                    apply(g, i - 1, 1)
                if old:
                    pe.wait_ge(hid_kept, after(g, i - 2, 1))
                    if i % GROUP == 2:
                        pe.wait_ge(w_f2, layer_of(g, i - 2) * 16 + 16)
                    if nxt:
                        pe.wait_ge(hT_kept, after(g, i + 1, 1))
                    for c in range(FILT // P):
                        last = mm(M2[:, 0:P], hid[:, i % 2, c, :], wf2[:, c, :], start=c == 0, stop=c == FILT // P - 1)
                    last.then_inc(f2_done, 1)
                if cur:
                    turn(g, i, 0)
                    scores(g, i, 1)
                if nxt:
                    values(g, i + 1, 1)
                if prev:
                    pe.wait_ge(o_kept, after(g, i - 1, 2, 1))
                    if i % GROUP == 1:
                        pe.wait_ge(w_o, layer_of(g, i - 1) * 16 + 16)
                    if nxt:
                        pe.wait_ge(hT_kept, after(g, i + 1, 1))
                    wait(pe, resid2, after(g, i - 2, 1))
                    for j in range(PAIRS):
                        last = mm(M2[:, 0:P], oT[:, (i - 1) % 2, j, :], wo[:, j, :], start=j == 0, stop=j == PAIRS - 1)
                    last.then_inc(wo_done, 1)
                if cur:
                    turn(g, i, 1)
                if nxt:
                    queries(g, i + 1, 0)
                    queries(g, i + 1, 1)
                if cur:
                    apply(g, i, 0)

            walk(pe, step)

            pe.wait_ge(resid2, UNITS)
            pe.wait_ge(f_in, 8 * 16)

            def f_scores(g, i, c):
                if c == 0:
                    pe.wait_ge(fq_kept, after(g, i, 1))
                    pe.wait_ge(fk_kept, after(g, i, 1))
                wait(pe, fexp, after(g, i, 4, c - 2))
                rows = slice(32 * c, 32 * c + 32)
                for j in range(ROW_HEADS):
                    last = mm(L[c % 2][:, j * P:(j + 1) * P], qm[rows, i % 2, j, :], kF[rows, i % 2, :], start=True, stop=True)
                last.then_inc(fqk, 1)

            def f_turn(g, i, c):
                pe.wait_ge(fexp, after(g, i, 4, c))
                wait(pe, fT_kept, after(g, i, 4, c - 2))
                for j in range(ROW_HEADS):
                    last = nc.tensor.transpose(T[c % 2][:, j * P:(j + 1) * P], prob[:, c, j, :], ident[:, :])
                last.then_inc(fT, 1)

            def f_apply(g, i):
                pe.wait_ge(fT_kept, after(g, i, 4, 3))
                pe.wait_ge(fv_kept, after(g, i, 1))
                wait(pe, fatt, after(g, i - 1, 1))
                for n in range(E_HEADS):
                    last = mm(O[:, n * VA:(n + 1) * VA], probT[:, n // 4, (n % 4) * P:(n % 4 + 1) * P], vF[:, i % 2, n, :],
                              start=True, stop=True)
                last.then_inc(fpv, 1)

            def f_step(g, i):
                nxt, cur, prev = f_there(g, i + 1), f_there(g, i), f_there(g, i - 1)
                if cur:
                    f_scores(g, i, 0)
                    f_scores(g, i, 1)
                if prev:
                    f_turn(g, i - 1, 2)
                    f_turn(g, i - 1, 3)
                    pe.wait_ge(fg_comb, after(g, i - 1, 1))
                    wait(pe, facc, after(g, i - 2, 1))
                    nc.tensor.transpose(M2[:, 0:P], comb[:, (i - 1) % 2, :], ident[:, :]).then_inc(fcT, 1)
                    for a, bank_ in enumerate((M0, M1)):
                        if a == 0:
                            pe.wait_ge(fq_kept, after(g, i if cur else i - 1, 1))
                            pe.wait_ge(fv_kept, after(g, i if cur else i - 1, 1))
                            pe.wait_ge(fg_kept, after(g, i if cur else i - 1, 1))
                        mm(bank_[:, :], hFT[:, (i - 1) % 2, :], we[:, 4 * a:4 * a + 4, :], start=True, stop=True).then_inc(fex, 1)
                    pe.wait_ge(fcT_kept, after(g, i - 1, 1))
                    mm(M2[:, 0:P], combT[:, (i - 1) % 2, :], be[:, :], start=True, stop=True).then_inc(fbe, 1)
                    f_apply(g, i - 1)
                if cur:
                    f_turn(g, i, 0)
                    f_scores(g, i, 2)
                    f_turn(g, i, 1)
                    f_scores(g, i, 3)
                if nxt:
                    pe.wait_ge(fh, after(g, i + 1, 1))
                    wait(pe, facc, after(g, i - 1, 1))
                    nc.tensor.transpose(M2[:, 0:P], hF[:, (i + 1) % 2, :], ident[:, :]).then_inc(fhT_done, 1)
                    pe.wait_ge(fhT_kept, after(g, i + 1, 1))
                    src = hFT[:, (i + 1) % 2, :]
                    mm(M0[:, 0:P], wqk[:, 0:P], src, start=True, stop=True).then_inc(fq_done, 1)
                    mm(M2[:, 0:P], wqk[:, P:2 * P], src, start=True, stop=True).then_inc(fk_done, 1)
                    mm(M1[:, 0:P + EXPERTS], src, wvg[:, :], start=True, stop=True).then_inc(fv_done, 1)

            walk(pe, f_step, F_GROUPS, 1, 1)

        @block.scalar
        def _(act):
            copy = ACT.Copy
            act.wait_ge(consts, 3)
            for n in range(BATCHES // 4):
                act.wait_ge(cT_done, n + 1)
                nc.scalar.activation(ctxT_all[:, 4 * n:4 * n + 4, :], T[n % 2][:, :], copy).then_inc(cT_kept, 1)

            def relu(g, k):
                if k == 0:
                    act.wait_ge(dist_in, (g + 1) * 32)
                wait(act, term_done, g * VEC_K + k + 1 - Z_SLOTS)
                nc.scalar.activation(relu_z[:, k % Z_SLOTS, :], dist_g[:, :, :], ACT.Relu, bias=cst[:, C_BTH + k:C_BTH + k + 1],
                                     scale=cst[:, C_WTH + k:C_WTH + k + 1]).then_inc(z_done, 1)

            def relus(g, i, q):
                if there(g, GROUP):
                    for k in Z_PLAN[i][q] if 0 <= i < GROUP else ():
                        relu(g + 1, k)

            def exps(g, i, c):
                act.wait_ge(scored, after(g, i, 4, c))
                wait(act, pT_done, after(g, i - 1, 4, c))
                wait(act, inv_done, after(g, i - 1, 4, c))
                for m in range(4):
                    last = nc.scalar.activation(prob[:, c, m, :], score[:, c, m, :], ACT.Exp, bias=nmax[:, c, m:m + 1],
                                                scale=-1.0, accum_out=rsum[:, c, m:m + 1])
                last.then_inc(exp_done, 1)

            def keep_turned(g, i, c):
                act.wait_ge(pT_done, after(g, i, 4, c))
                wait(act, pv_done, after(g, i - 1, 2, c // 2))
                nc.scalar.activation(probT[:, c, :], T[0][:, :], copy).then_inc(pT_even, 1)

            def keep_o(g, i, octet):
                act.wait_ge(pv_done, after(g, i, 2, octet))
                wait(act, wo_done, after(g, i - 2, 1))
                nc.scalar.activation(oT[:, i % 2, 4 * octet:4 * octet + 4, :], O[:, :], copy).then_inc(o_kept, 1)

            for k in range(VEC_K):
                relu(0, k)

            def step(g, i):
                nxt, cur, prev = there(g, i + 1), there(g, i), there(g, i - 1)
                if prev:
                    keep_turned(g, i - 1, 2)
                if nxt:
                    act.wait_ge(k_done, after(g, i + 1, 2, 0))
                    wait(act, qk_done, after(g, i - 1, 4, 3))
                    nc.scalar.activation(kT[:, (i + 1) % 2, 0:4, :], M0[:, :], copy).then_inc(k_kept[0], 1)
                relus(g, i, 0)
                if cur:
                    exps(g, i, 0)
                relus(g, i, 1)
                if nxt:
                    act.wait_ge(v_done, after(g, i + 1, 2, 0))
                    wait(act, pv_done, after(g, i - 1, 2, 1))
                    nc.scalar.activation(v[:, (i + 1) % 2, 0:512], M1[:, :], copy).then_inc(v_kept[0], 1)
                if cur:
                    exps(g, i, 1)
                if prev:
                    keep_o(g, i - 1, 1)
                if cur:
                    keep_turned(g, i, 0)
                relus(g, i, 2)
                if cur:
                    exps(g, i, 2)
                relus(g, i, 3)
                if cur:
                    exps(g, i, 3)
                if nxt:
                    act.wait_ge(q_done, after(g, i + 1, 2, 0))
                    wait(act, qk_done, after(g, i - 1, 4, 3))
                    nc.scalar.activation(qT[:, (i + 1) % 2, 0:4, :], M0[:, :], copy, scale=HD ** -0.5).then_inc(q_kept[0], 1)
                if cur:
                    keep_o(g, i, 0)

            walk(act, step)

            act.wait_ge(resid2, UNITS)
            act.wait_ge(f_gate_in, 32)
            nc.scalar.activation(tg[:, :], gates_in[:, :], ACT.Tanh).then_inc(tanh_done, 1)
            act.wait_ge(f_in, 8 * 16)

            def f_exps(g, i, c):
                act.wait_ge(fmax, after(g, i, 4, c))
                wait(act, fT, after(g, i - 1, 4, c))
                for j in range(4):
                    last = nc.scalar.activation(prob[:, c, j, :], L[c % 2][:, j * P:(j + 1) * P], ACT.Exp,
                                                bias=nmaxF[:, c, j:j + 1], scale=1.0)
                last.then_inc(fexp, 1)

            def f_keep(g, i, c):
                act.wait_ge(fT, after(g, i, 4, c))
                wait(act, fpv, after(g, i - 1, 1))
                nc.scalar.activation(probT[:, c, :], T[c % 2][:, :], copy).then_inc(fT_kept, 1)

            def f_step(g, i):
                nxt, cur, prev = f_there(g, i + 1), f_there(g, i), f_there(g, i - 1)
                if cur:
                    f_exps(g, i, 0)
                if prev:
                    f_keep(g, i - 1, 2)
                    f_keep(g, i - 1, 3)
                if cur:
                    f_exps(g, i, 1)
                    f_keep(g, i, 0)
                    f_exps(g, i, 2)
                    f_keep(g, i, 1)
                    f_exps(g, i, 3)
                if nxt:
                    act.wait_ge(fk_done, after(g, i + 1, 1))
                    wait(act, fqk, after(g, i - 1, 4, 3))
                    nc.scalar.activation(kF[:, (i + 1) % 2, :], M2[:, 0:P], ACT.Identity, bias=bqk[:, 1:2]).then_inc(fk_kept, 1)
                    a = (i + 1) % 2
                    act.wait_ge(fg_neg, after(g, i + 1, 1))
                    wait(act, fg_inv, after(g, i - 1, 1))
                    nc.scalar.activation(gate[:, a, 1, :], gate[:, a, 0, :], ACT.Exp, bias=gsum[:, a, 1:2], scale=1.0,
                                         accum_out=gsum[:, a, 0:1]).then_inc(fg_exp, 1)

            walk(act, f_step, F_GROUPS, 1, 1)

        @block.vector
        def _(dve):
            vec = nc.vector
            dve.wait_ge(consts, 3)
            def cols(a):
                return cst_all[:, :, a:a + BIAS_K]

            dve.wait_ge(cst_in, 64)
            vec.tensor_tensor(cols(C_PW), cols(C_WTH), cols(C_WTO), ALU.mult).then_inc(cst_ready, 1)
            vec.tensor_tensor(cols(C_PB), cols(C_BTH), cols(C_WTO), ALU.mult).then_inc(cst_ready, 1)
            vec.tensor_scalar(cols(C_HI), cols(C_WTO), 0.0, BIG, ALU.is_ge, ALU.mult).then_inc(cst_ready, 1)
            vec.tensor_scalar(cols(C_LO), cols(C_WTO), 0.0, -BIG, ALU.is_le, ALU.mult).then_inc(cst_ready, 1)
            dve.wait_ge(x_in, 16)
            for b in range(BATCHES):
                vec.bn_stats(ln_st[:, b, :], x_raw[:, b, :]).then_inc(ln_bn, 1)
            for b in range(BATCHES):
                dve.wait_ge(ln_bn, b + 1)
                vec.bn_aggr(ln_mv[:, b, :], ln_st[:, b, :]).then_inc(ln_mvd, 1)
            dve.wait_ge(ln_mvd, BATCHES)
            vec.tensor_scalar(ln_ve[:, :], ln_mv[:, :, 1], LN_EPS, None, ALU.add).then_inc(ln_vd, 1)
            dve.wait_ge(ln_sdd, 1)
            vec.reciprocal(ln_rs[:, :], ln_sd[:, :]).then_inc(ln_rd, 1)
            dve.wait_ge(ln_rd, 1)
            for b in range(BATCHES):
                vec.tensor_scalar(x_all[:, b, :], x_raw[:, b, :], ln_mv[:, b, 0:1], ln_rs[:, b:b + 1],
                                  ALU.subtract, ALU.mult).then_inc(ln_done, 1)

            def term(g, k):
                if k == 0:
                    dve.wait_ge(cv_in, (g + 1) * 32)
                    wait(dve, bias_done, g)
                else:
                    dve.wait_ge(term_done, g * VEC_K + k)
                dve.wait_ge(z_done, g * VEC_K + k + 1)
                weight = cst[:, C_WTO + k:C_WTO + k + 1]
                if k == 0:
                    vec.tensor_scalar(bias_acc[:, :], relu_z[:, 0, :], weight, cst[:, C_BTO:C_BTO + 1], ALU.mult,
                                      ALU.add).then_inc(term_done, 1)
                else:
                    vec.scalar_tensor_tensor(out=bias_acc[:, :], in0=relu_z[:, k % Z_SLOTS, :], scalar=weight,
                                             in1=bias_acc[:, :], op0=ALU.mult, op1=ALU.add).then_inc(term_done, 1)

            def terms(g, i, q):
                if there(g, GROUP):
                    for k in TERM_PLAN[i][q] if 0 <= i < GROUP else ():
                        term(g + 1, k)

            def finish_bias(g, i):
                dve.wait_ge(pool_sum, (g + 1) * POOL_K)
                dve.wait_ge(term_done, (g + 1) * VEC_K)
                wait(dve, scored, after(g, -1, 4, 3))
                vec.tensor_tensor(bias[:, :, :], bias_acc[:, :].rearrange("p (b t) -> p b t", b=GROUP),
                                  pool_acc[:, :, :], ALU.add).then_inc(bias_done, 1)

            def score_quad(g, i, c):
                for m in range(4):
                    if m == 0:
                        if i % GROUP == 0 and c == 0:
                            dve.wait_ge(bias_done, g + i // GROUP + 1)
                        wait_first(dve, consts, qk_done, after(g, i, 4, c), exp_done, after(g, i - 1, 4, c))
                    last = vec.tensor_tensor_reduce(out=score[:, c, m, :], in0=L[c % 2][:, m * P:(m + 1) * P], in1=bias[:, i % GROUP, :],
                                                    scale=-1.0, scalar=BIG, op0=ALU.add, op1=ALU.min,
                                                    accum_out=nmax[:, c, m:m + 1])
                last.then_inc(scored, 1)

            def inverse(g, i, c):
                dve.wait_ge(exp_done, after(g, i, 4, c))
                wait(dve, normed, after(g, i - 1, 4, c))
                vec.reciprocal(rinv[:, c, :], rsum[:, c, :]).then_inc(inv_done, 1)

            def moments(g, i, a):
                s = i % 2
                if a == 0:
                    dve.wait_ge(xs_in[i % GROUP], (g + i // GROUP) * 16 + 16)
                else:
                    dve.wait_ge(resid1, after(g, i, 1))
                wait(dve, h_done[a], after(g, i - 2, 1))
                vec.bn_stats(st[:, a, s, :], xs[:, i % GROUP, :]).then_inc(bn[a], 1)
                wait_first(dve, consts, bn[a], after(g, i, 1))
                vec.bn_aggr(mv[:, a, s, :], st[:, a, s, :]).then_inc(var[a], 1)

            def scale(g, i, a):
                s = i % 2
                dve.wait_ge(sdev[a], after(g, i, 1))
                vec.tensor_scalar(sde[:, a, s:s + 1], sd[:, a, s:s + 1], NORM_EPS, None, ALU.add).then_inc(sdeps[a], 1)
                dve.wait_ge(sdeps[a], after(g, i, 1))
                vec.reciprocal(rs[:, a, s:s + 1], sde[:, a, s:s + 1]).then_inc(rstd[a], 1)

            def normalise(g, i, a):
                s = i % 2
                dve.wait_ge(rstd[a], after(g, i, 1))
                wait(dve, h2T_done if a else hT_done, after(g, i - 2, 1))
                vec.tensor_scalar((h2 if a else h)[:, s, :], xs[:, i % GROUP, :], mv[:, a, s, 0:1], rs[:, a, s:s + 1],
                                  ALU.subtract, ALU.mult).then_inc(h_done[a], 1)

            def keep_turned(g, i, c):
                dve.wait_ge(pT_done, after(g, i, 4, c))
                wait(dve, pv_done, after(g, i - 1, 2, c // 2))
                vec.tensor_copy(probT[:, c, :], T[1][:, :]).then_inc(pT_odd, 1)

            for k in range(VEC_K):
                term(0, k)
            finish_bias(0, 0)
            moments(0, 0, 0)

            def step(g, i):
                nxt, cur, prev, old = there(g, i + 1), there(g, i), there(g, i - 1), there(g, i - 2)
                if prev:
                    inverse(g, i - 1, 3)
                terms(g, i, 0)
                if old:
                    dve.wait_ge(h2T_done, after(g, i - 2, 1))
                    wait(dve, f1_done, after(g, i - 4, 1))
                    vec.tensor_copy(h2T[:, i % 2, :], M2[:, 0:P]).then_inc(h2T_kept, 1)
                if nxt:
                    scale(g, i + 1, 0)
                    normalise(g, i + 1, 0)
                if cur:
                    score_quad(g, i, 0)
                if old:
                    for c in range(FILT // P):
                        if c == 0:
                            dve.wait_ge(f1_done, after(g, i - 2, 1))
                            wait(dve, f2_done, after(g, i - 4, 1))
                            if i % GROUP == 2:
                                dve.wait_ge(w_b1, layer_of(g, i - 2) * 16 + 16)
                        last = vec.tensor_scalar(hid[:, i % 2, c, :], M1[:, c * P:(c + 1) * P], bf1c[:, c:c + 1], 0.0, ALU.add, ALU.max)
                    last.then_inc(hid_kept, 1)
                if prev:
                    keep_turned(g, i - 1, 3)
                if nxt:
                    dve.wait_ge(hT_done, after(g, i + 1, 1))
                    wait(dve, q_done, after(g, i - 1, 2, 1))
                    vec.tensor_copy(hT[:, (i + 1) % 2, :], M2[:, 0:P]).then_inc(hT_kept, 1)
                if cur:
                    inverse(g, i, 0)
                    score_quad(g, i, 1)
                if nxt:
                    dve.wait_ge(k_done, after(g, i + 1, 2, 1))
                    wait(dve, qk_done, after(g, i - 1, 4, 3))
                    vec.tensor_copy(kT[:, (i + 1) % 2, 4:8, :], M0[:, :]).then_inc(k_kept[1], 1)
                terms(g, i, 1)
                if old:
                    dve.wait_ge(f2_done, after(g, i - 2, 1))
                    dve.wait_ge(xb_done, after(g, i - 2, 1))
                    vec.tensor_tensor(xs[:, (i - 2) % GROUP, :], M2[:, 0:P], xb[:, i % 2, :], ALU.add).then_inc(resid2, 1)
                if cur:
                    inverse(g, i, 1)
                terms(g, i, 2)
                if cur:
                    score_quad(g, i, 2)
                if nxt:
                    dve.wait_ge(v_done, after(g, i + 1, 2, 1))
                    wait(dve, pv_done, after(g, i - 1, 2, 1))
                    vec.tensor_copy(v[:, (i + 1) % 2, 512:1024], M0[:, :]).then_inc(v_kept[1], 1)
                if cur:
                    score_quad(g, i, 3)
                if prev:
                    dve.wait_ge(wo_done, after(g, i - 1, 1))
                    vec.tensor_tensor(xs[:, (i - 1) % GROUP, :], M2[:, 0:P], xs[:, (i - 1) % GROUP, :], ALU.add).then_inc(resid1, 1)
                if cur:
                    inverse(g, i, 2)
                    keep_turned(g, i, 1)
                if prev:
                    moments(g, i - 1, 1)
                terms(g, i, 3)
                if prev:
                    scale(g, i - 1, 1)
                    normalise(g, i - 1, 1)
                if nxt:
                    dve.wait_ge(q_done, after(g, i + 1, 2, 1))
                    wait(dve, qk_done, after(g, i - 1, 4, 3))
                    vec.tensor_scalar(qT[:, (i + 1) % 2, 4:8, :], M1[:, :].rearrange("p (a b) -> p a b", a=4), HD ** -0.5, None,
                                      ALU.mult).then_inc(q_kept[1], 1)
                if there(g, i + 2):
                    moments(g, i + 2, 0)
                if i == GROUP - 1 and there(g, GROUP):
                    finish_bias(g + 1, 0)

            walk(dve, step)

            dve.wait_ge(tanh_done, 1)
            dve.wait_ge(f_consts, 4)
            dve.wait_ge(f_in, 8 * 16)
            vec.tensor_reduce(head_mask[:, :], head_rows[:, :].rearrange("p (c j) -> p j c", j=ROW_HEADS), AX_X,
                              ALU.add).then_inc(f_consts, 1)
            dve.wait_ge(f_consts, 5)

            def f_stats(g, i, a):
                s = i % 2
                if a == 0:
                    dve.wait_ge(x4_in[i % GROUP], (g + i // GROUP) * 16 + 16)
                    wait(dve, fdelta, after(g, i - 2, 1))
                else:
                    dve.wait_ge(fx1, after(g, i, 1))
                    wait(dve, fh, after(g, i - 2, 1))
                vec.bn_stats(stF[:, a, s, :], (x1 if a else x4)[:, i % GROUP, :]).then_inc(fbn[a], 1)
                wait_first(dve, consts, fbn[a], after(g, i, 1))
                vec.bn_aggr(mvF[:, a, s, :], stF[:, a, s, :]).then_inc(fvar[a], 1)
                if a == 1:
                    dve.wait_ge(fvar[1], after(g, i, 1))
                    vec.tensor_scalar(tinyF[:, s, 4:5], mvF[:, 1, s, 1:2], LN_EPS, None, ALU.add).then_inc(fve[1], 1)

            def f_first(g, i):
                s = i % 2
                t = tinyF[:, s, :]
                dve.wait_ge(fsd[0], after(g, i, 1))
                vec.tensor_scalar(t[:, 1:2], t[:, 0:1], NORM_EPS, None, ALU.add).then_inc(fsde[0], 1)
                dve.wait_ge(fsde[0], after(g, i, 1))
                vec.reciprocal(t[:, 2:3], t[:, 1:2]).then_inc(frs[0], 1)
                dve.wait_ge(frs[0], after(g, i, 1))
                vec.tensor_tensor(t[:, 3:4], t[:, 2:3], tg[:, 0:1], ALU.mult).then_inc(frg[0], 1)
                dve.wait_ge(frg[0], after(g, i, 1))
                wait(dve, fx1, after(g, i - 2, 1))
                vec.tensor_scalar(delta[:, s, :], x4[:, i % GROUP, :], mvF[:, 0, s, 0:1], t[:, 3:4], ALU.subtract,
                                  ALU.mult).then_inc(fdelta, 1)
                dve.wait_ge(xr_in[i % GROUP], (g + i // GROUP) * 16 + 16)
                dve.wait_ge(fdelta, after(g, i, 1))
                wait(dve, fout, after(g, i - GROUP, 1))
                vec.tensor_tensor(x1[:, i % GROUP, :], delta[:, s, :], xr[:, i % GROUP, :], ALU.add).then_inc(fx1, 1)

            def f_norm(g, i):
                s = i % 2
                t = tinyF[:, s, :]
                dve.wait_ge(fsd[1], after(g, i, 1))
                vec.reciprocal(t[:, 6:7], t[:, 5:6]).then_inc(frs[1], 1)
                dve.wait_ge(frs[1], after(g, i, 1))
                wait(dve, fhT_done, after(g, i - 2, 1))
                vec.tensor_scalar(hF[:, s, :], x1[:, i % GROUP, :], mvF[:, 1, s, 0:1], t[:, 6:7], ALU.subtract,
                                  ALU.mult).then_inc(fh, 1)

            def f_max(g, i, c):
                dve.wait_ge(fqk, after(g, i, 4, c))
                wait(dve, fexp, after(g, i - 1, 4, c))
                vec.tensor_reduce(nmaxF[:, c, :], L[c % 2][:, :].rearrange("p (j t) -> p j t", j=4), AX_X, ALU.max,
                                  negate=True).then_inc(fmax, 1)

            def f_gate_logits(g, i):
                s = i % 2
                dve.wait_ge(fv_done, after(g, i, 1))
                wait(dve, fg_exp, after(g, i - 2, 1))
                vec.tensor_tensor(gate[:, s, 0, :], M1[:, P:P + EXPERTS], bvg[:, P:P + EXPERTS], ALU.add).then_inc(fg_kept, 1)
                wait(dve, fpv, after(g, i - 2, 1))
                vec.tensor_tensor(vF[:, s, :, 0:E_HD], M1[:, 0:P].rearrange("p (n e) -> p n e", n=E_HEADS),
                                  bvg[:, 0:P].rearrange("p (n e) -> p n e", n=E_HEADS), ALU.add).then_inc(fv_kept, 1)
                wait_first(dve, consts, fg_kept, after(g, i, 1), fg_idx, after(g, i - 2, 1))
                vec.max(gate[:, s, 2, :], gate[:, s, 0, :]).then_inc(fg_top, 1)
                dve.wait_ge(fg_top, after(g, i, 1))
                wait(dve, fg_exp, after(g, i - 2, 1))
                vec.tensor_scalar(gsum[:, s, 1:2], gate[:, s, 2, 0:1], -1.0, None, ALU.mult).then_inc(fg_neg, 1)

            def f_gates(g, i):
                s = i % 2
                dve.wait_ge(fg_exp, after(g, i, 1))
                vec.reciprocal(tinyF[:, s, 7:8], gsum[:, s, 0:1]).then_inc(fg_inv, 1)
                dve.wait_ge(fg_inv, after(g, i, 1))
                wait(dve, fg_idx, after(g, i - 2, 1))
                vec.tensor_scalar(gate[:, s, 3, :], gate[:, s, 1, :], tinyF[:, s, 7:8], None, ALU.mult).then_inc(fg_soft, 1)
                wait_first(dve, consts, fg_neg, after(g, i, 1), fg_soft, after(g, i, 1))
                vec.max(gate[:, s, 2, :], gate[:, s, 3, :]).then_inc(fg_top2, 1)
                wait_first(dve, consts, fg_top2, after(g, i, 1))
                vec.max_index(topi[:, s, :], gate[:, s, 2, :], gate[:, s, 3, :]).then_inc(fg_idx, 1)
                dve.wait_ge(fg_idx, after(g, i, 1))
                vec.tensor_copy(gate[:, s, 0, 0:2], topi[:, s, 0:2]).then_inc(fg_idxf, 1)
                dve.wait_ge(fg_idxf, after(g, i, 1))
                vec.tensor_scalar(gate[:, s, 4, :], eidx[:, :], gate[:, s, 0, 0:1], gate[:, s, 2, 0:1], ALU.is_equal,
                                  ALU.mult).then_inc(fg_c0, 1)
                vec.tensor_scalar(gate[:, s, 1, :], eidx[:, :], gate[:, s, 0, 1:2], gate[:, s, 2, 1:2], ALU.is_equal,
                                  ALU.mult).then_inc(fg_c1, 1)
                dve.wait_ge(fg_c0, after(g, i, 1))
                dve.wait_ge(fg_c1, after(g, i, 1))
                wait(dve, facc, after(g, i - 2, 1))
                wait(dve, fcT, after(g, i - 2, 1))
                vec.tensor_tensor(comb[:, s, 0:EXPERTS], gate[:, s, 4, :], gate[:, s, 1, :], ALU.add).then_inc(fg_comb, 1)

            def f_sum(g, i):
                s = i % 2
                dve.wait_ge(fpv, after(g, i, 1))
                o = O[:, 0:E_HEADS * VA].rearrange("p (n e) -> p n e", e=VA)
                wait(dve, fatt, after(g, i - 1, 1))
                vec.reciprocal(rinvF[:, :], o[:, :, E_HD]).then_inc(fsums, 1)
                dve.wait_ge(fsums, after(g, i, 1))
                wait(dve, fout, after(g, i - 1, 1))
                vec.tensor_tensor(accF[:, :].rearrange("p (n e) -> p n e", n=E_HEADS), o[:, :, 0:E_HD],
                                  rinvF[:, :].rearrange("p (n o) -> p n o", o=1).broadcast_to([P, E_HEADS, E_HD]),
                                  ALU.mult).then_inc(fatt, 1)
                dve.wait_ge(fatt, after(g, i, 1))
                dve.wait_ge(fbe, after(g, i, 1))
                vec.tensor_tensor(accF[:, :], M2[:, 0:P], accF[:, :], ALU.add).then_inc(fex_acc, 1)
                for e in range(EXPERTS):
                    if e % 4 == 0:
                        dve.wait_ge(fex, after(g, i, 2, e // 4))
                    dve.wait_ge(fex_acc, after(g, i, EXPERTS, e))
                    last = vec.scalar_tensor_tensor(out=accF[:, :], in0=(M1 if e >= 4 else M0)[:, (e % 4) * P:(e % 4 + 1) * P],
                                                    scalar=comb[:, s, e:e + 1], in1=accF[:, :], op0=ALU.mult, op1=ALU.add)
                    last.then_inc(facc if e == EXPERTS - 1 else fex_acc, 1)
                dve.wait_ge(facc, after(g, i, 1))
                wait(dve, out_st[s], (g * 2 + i // 2) * 16)
                vec.scalar_tensor_tensor(out=outF[:, s, :], in0=accF[:, :], scalar=tg[:, 1:2], in1=x1[:, i % GROUP, :],
                                         op0=ALU.mult, op1=ALU.add).then_inc(fout, 1)

            def f_step(g, i):
                far, nxt, cur, prev = f_there(g, i + 2), f_there(g, i + 1), f_there(g, i), f_there(g, i - 1)
                if cur:
                    f_max(g, i, 0)
                if nxt:
                    f_norm(g, i + 1)
                if cur:
                    f_max(g, i, 1)
                if prev:
                    dve.wait_ge(fcT, after(g, i - 1, 1))
                    wait(dve, fbe, after(g, i - 3, 1))
                    vec.tensor_copy(combT[:, (i - 1) % 2, :], M2[0:EXPERTS, 0:P]).then_inc(fcT_kept, 1)
                if far:
                    f_stats(g, i + 2, 0)
                if cur:
                    f_max(g, i, 2)
                if prev:
                    f_sum(g, i - 1)
                if cur:
                    f_max(g, i, 3)
                if far:
                    f_first(g, i + 2)
                    f_stats(g, i + 2, 1)
                if nxt:
                    dve.wait_ge(fhT_done, after(g, i + 1, 1))
                    wait(dve, fex, after(g, i - 1, 2, 1))
                    vec.tensor_copy(hFT[:, (i + 1) % 2, :], M2[:, 0:P]).then_inc(fhT_kept, 1)
                    dve.wait_ge(fq_done, after(g, i + 1, 1))
                    wait(dve, fqk, after(g, i - 1, 4, 3))
                    for j in range(ROW_HEADS):
                        last = vec.tensor_scalar(qm[:, (i + 1) % 2, j, :], M0[:, 0:P], bqk[:, 0:1], head_mask[:, j:j + 1],
                                                 ALU.add, ALU.mult)
                    last.then_inc(fq_kept, 1)
                    f_gate_logits(g, i + 1)
                    f_gates(g, i + 1)

            walk(dve, f_step, F_GROUPS, 2, 1)

        @block.gpsimd
        def _(pool):
            gp = nc.gpsimd
            gp.memset(half[:, :], 0.5).then_inc(consts, 1)
            gp.memset(ident[:, :], 0.0).then_inc(consts, 1)
            pool.wait_ge(consts, 2)
            gp.affine_select(out=ident[:, :], in_=ident[:, :], compare_op=ALU.not_equal, fill=1.0, base=0,
                             pattern=[[-1, P]], channel_multiplier=1).then_inc(consts, 1)
            pool.wait_ge(ln_vd, 1)
            gp.tensor_tensor(ln_sd[:, :], ln_ve[:, :], half[:, :], ALU.pow).then_inc(ln_sdd, 1)

            def root(g, i, a):
                s = i % 2
                pool.wait_ge(var[a], after(g, i, 1))
                wait(pool, sdeps[a], after(g, i - 2, 1))
                gp.tensor_tensor(sd[:, a, s:s + 1], mv[:, a, s, 1:2], half[:, 0:1], ALU.pow).then_inc(sdev[a], 1)

            def norm(g, i, c):
                pool.wait_ge(inv_done, after(g, i, 4, c))
                gp.tensor_tensor(prob[:, c, :, :], prob[:, c, :, :],
                                 rinv[:, c, :].rearrange("p (m o) -> p m o", o=1).broadcast_to([P, 4, P]),
                                 ALU.mult).then_inc(normed, 1)

            def product(g, k):
                col = VEC_K + k
                wait_first(pool, consts, *((dist_in, (g + 1) * 32, cp_in, (g + 1) * 16) if k == 0 else ()),
                           pool_clamp, g * POOL_K + k - 1)
                gp.tensor_scalar(clamp_in[:, k % 2, :], dist_g[:, :, :], cst[:, C_PW + col:C_PW + col + 1],
                                 cst[:, C_PB + col:C_PB + col + 1], ALU.mult, ALU.add).then_inc(pool_mul, 1)

            def clamp(g, k):
                col = VEC_K + k
                wait_first(pool, consts, pool_mul, g * POOL_K + k + 1, pool_sum, g * POOL_K + k - 1)
                gp.tensor_scalar(clamped[:, k % 2, :], clamp_in[:, k % 2, :], cst[:, C_HI + col:C_HI + col + 1],
                                 cst[:, C_LO + col:C_LO + col + 1], ALU.min, ALU.max).then_inc(pool_clamp, 1)

            def add(g, k):
                pool.wait_ge(pool_clamp, g * POOL_K + k + 1)
                if k == 0:
                    pool.wait_ge(cv_in, (g + 1) * 32)
                    wait(pool, bias_done, g)
                else:
                    pool.wait_ge(pool_sum, g * POOL_K + k)
                so_far = mask_g if k == 0 else pool_acc
                gp.tensor_tensor(pool_acc[:, :, :], so_far[:, :, :], clamped[:, k % 2, :].rearrange("p (b t) -> p b t", b=GROUP),
                                 ALU.add).then_inc(pool_sum, 1)

            def step(g, i):
                nxt, cur, prev = there(g, i + 1), there(g, i), there(g, i - 1)
                if nxt:
                    root(g, i + 1, 0)
                if prev:
                    norm(g, i - 1, 3)
                bias_too = 0 <= i < GROUP and there(g, GROUP)
                if bias_too:
                    product(g + 1, 2 * i)
                    clamp(g + 1, 2 * i)
                if cur:
                    norm(g, i, 0)
                if bias_too:
                    add(g + 1, 2 * i)
                    product(g + 1, 2 * i + 1)
                if cur:
                    norm(g, i, 1)
                if bias_too:
                    clamp(g + 1, 2 * i + 1)
                    add(g + 1, 2 * i + 1)
                if cur:
                    norm(g, i, 2)
                if prev:
                    root(g, i - 1, 1)
                    pool.wait_ge(resid1, after(g, i - 1, 1))
                    wait(pool, resid2, after(g, i - 3, 1))
                    if i % GROUP == 1:
                        pool.wait_ge(w_b2, layer_of(g, i - 1) * 16 + 16)
                    gp.tensor_tensor(xb[:, (i - 1) % 2, :], xs[:, (i - 1) % GROUP, :], bf2b[:, :], ALU.add).then_inc(xb_done, 1)

            for k in range(POOL_K):
                product(0, k)
                clamp(0, k)
                add(0, k)

            gp.memset(head_rows[:, :], E_HD ** -0.5).then_inc(f_prep, 1)
            gp.memset(comb[:, :, :], 0.0).then_inc(f_consts, 1)
            gp.memset(vF[:, :, :, :], 1.0).then_inc(f_consts, 1)
            gp.iota(eidx[:, :], pattern=[[1, EXPERTS]], base=0, channel_multiplier=0,
                    allow_small_or_imprecise_dtypes=True).then_inc(f_consts, 1)
            pool.wait_ge(f_prep, 1)
            gp.affine_select(out=head_rows[:, :], in_=head_rows[:, :], compare_op=ALU.is_ge, fill=0.0, base=0,
                             pattern=[[-E_HD, E_HEADS]], channel_multiplier=1).then_inc(f_prep, 1)
            pool.wait_ge(f_prep, 2)
            gp.affine_select(out=head_rows[:, :], in_=head_rows[:, :], compare_op=ALU.is_ge, fill=0.0, base=E_HD - 1,
                             pattern=[[E_HD, E_HEADS]], channel_multiplier=-1).then_inc(f_consts, 1)

            walk(pool, step)

            def f_step(g, i):
                for a, d in ((1, 1), (0, 2)):
                    if f_there(g, i + d):
                        s = i % 2 if d == 2 else (i + 1) % 2
                        if a == 1:
                            pool.wait_ge(fve[1], after(g, i + d, 1))
                            wait(pool, frs[1], after(g, i + d - 2, 1))
                            gp.tensor_tensor(tinyF[:, s, 5:6], tinyF[:, s, 4:5], half[:, 0:1], ALU.pow).then_inc(fsd[1], 1)
                        else:
                            pool.wait_ge(fvar[0], after(g, i + d, 1))
                            wait(pool, fsde[0], after(g, i + d - 2, 1))
                            gp.tensor_tensor(tinyF[:, s, 0:1], mvF[:, 0, s, 1:2], half[:, 0:1], ALU.pow).then_inc(fsd[0], 1)

            walk(pool, f_step, F_GROUPS, 2, 1)


_INS = ["x", "ctx_1024", "fside_BxSxS2_0", "mask_Bx1x1xS2_ff0", "g_xattn", "g_ffn", "L0_xattn_Wq", "L0_xattn_Wk",
        "L0_xattn_Wv", "L0_xattn_Wo", "L0_xattn_Wth", "L0_xattn_bth", "L0_xattn_Wto", "L0_xattn_bto", "L0_xattn_Wf1",
        "L0_xattn_bf1", "L0_xattn_Wf2", "L0_xattn_bf2", "L0_ffn_W_qkv", "L0_ffn_b_qkv", "L0_ffn_W_gate", "L0_ffn_b_gate",
        "L0_ffn_W_experts", "L0_ffn_b_experts"]


def kernel(**inputs):
    import concourse.bacc as _bacc
    from concourse.bass_utils import run_bass_kernel_spmd as _run

    nc = _bacc.Bacc("TRN2", target_bir_lowering=False, num_devices=1)
    arrays, args = {}, []
    for name in _INS:
        a = np.ascontiguousarray(inputs[name])
        arrays[f"in_{name}"] = a
        args.append(nc.dram_tensor(f"in_{name}", a.shape, mybir.dt.from_np(a.dtype), kind="ExternalInput").ap())
    shape = (BATCHES, P, P)
    args.append(nc.dram_tensor("out_0", shape, F32, kind="ExternalOutput").ap())
    block_program(nc, *args)
    r = _run(nc, [arrays], core_ids=[0])
    return r.results[0]["out_0"]
```

```python
from contextlib import ExitStack

import numpy as np
import concourse.bass as bass
from concourse import mybir

F32 = mybir.dt.float32
U32 = mybir.dt.uint32
ALU = mybir.AluOpType
ACT = mybir.ActivationFunctionType
AX_X = mybir.AxisListType.X

P = 128
BATCHES = 16
LAYERS = 4
HEADS = 16
HD = 64
BIAS_K = 32
FILT = 512
GROUP = 4
UNITS = LAYERS * BATCHES
GROUPS = UNITS // GROUP
GROUPS_PER_LAYER = BATCHES // GROUP
QUADS = 4
PAIRS = HEADS // 2
NORM_EPS = 1e-6
LN_EPS = 1e-5
BIG = 3.0e38

VEC_K = 24
POOL_K = BIAS_K - VEC_K
START_VEC_K = 26
START_POOL_SKIP = START_VEC_K - VEC_K
POOL_FIRST = 2
Z_SLOTS = 6
assert VEC_K % Z_SLOTS == 0


def plan(counts):
    ends = np.cumsum(np.array(counts).ravel()).reshape(np.shape(counts))
    return [[list(range(int(e) - n, int(e))) for n, e in zip(row, ends_)] for row, ends_ in zip(counts, ends)]


Z_PLAN = plan([[1, 2, 2, 1, 0], [1, 2, 2, 1, 0], [1, 2, 2, 1, 0], [2, 2, 2, 0, 0]])
TERM_PLAN = plan([[0, 2, 1, 1, 1], [1, 2, 1, 1, 1], [1, 2, 1, 1, 1], [1, 2, 2, 1, 1]])
assert sum(map(len, sum(Z_PLAN, []))) == sum(map(len, sum(TERM_PLAN, []))) == VEC_K and POOL_K == 2 * GROUP
START_Z = plan([[2, 3, 4, 2, 4]])[0]
START_TERMS = plan([[2, 3, 4, 2, 4]])[0]
Z_BEFORE = START_VEC_K - 1 - START_Z[-1][-1]
TERMS_BEFORE = START_VEC_K - 1 - START_TERMS[-1][-1]
STATS_TERMS = (4, 8)
EARLY_STEPS = (1, 2)
F_FIRST_PARTS = [[0, 1], [2, 3, 4], [5, 6], [7, 8, 9], [10, 11]]


def vec_count(g, k):
    return k if isinstance(g, int) and g == 0 else g * VEC_K + (START_VEC_K - VEC_K + k)


def pool_count(g, k):
    return k - START_POOL_SKIP if isinstance(g, int) and g == 0 else g * POOL_K + (k - START_POOL_SKIP)


def z_slot(g, k):
    return (k if isinstance(g, int) and g == 0 else START_VEC_K + k) % Z_SLOTS


C_WTH, C_BTH, C_WTO = 0, BIAS_K, 2 * BIAS_K
C_BTO = 3 * BIAS_K
C_PW, C_PB, C_HI, C_LO = [C_BTO + 1 + n * BIAS_K for n in range(4)]
C_ALL = C_BTO + 1 + 4 * BIAS_K

E_HEADS = 16
E_HD = 8
EXPERTS = 8
ROW_HEADS = 4
F_GROUPS = BATCHES // GROUP
VA = 32


def wait(eng, sem, value):
    if isinstance(value, int) and value < 1:
        return
    eng.wait_ge(sem, value)


def wait_first(eng, consts, *counts):
    pairs = [(s, v) for s, v in zip(counts[::2], counts[1::2]) if not isinstance(v, int) or v > 0]
    pairs = [(s, v if isinstance(v, int) else eng.to_reg(v)) for s, v in pairs]
    eng.wait_ge(consts, 3)
    for s, v in pairs:
        eng.wait_ge(s, v)


def after(g, i, per, k=0):
    return g * (GROUP * per) + (i * per + k + 1)


def block_program(nc, x, ctx_in, dist, mask, g_xattn, g_ffn, Wq, Wk, Wv, Wo, Wth, bth, Wto, bto,
                  Wf1, bf1, Wf2, bf2, W_qkv, b_qkv, W_gate, b_gate, W_experts, b_experts, out):
    with ExitStack() as stack:
        def sb(name, shape, dt=F32):
            return stack.enter_context(nc.sbuf_tensor(name, shape, dt))

        def sem(name):
            return stack.enter_context(nc.semaphore(name))

        ident = sb("ident", [P, P])
        half = sb("half", [P, BATCHES])
        tables = sb("tables", [P, 1])
        x_raw = sb("x_raw", [P, BATCHES, P])
        c_raw = sb("c_raw", [P, BATCHES, P])
        x_all = sb("x_all", [P, BATCHES, P])
        ctxT_all = sb("ctxT_all", [P, BATCHES, P])
        ln_st = sb("ln_st", [P, BATCHES, 6])
        ln_mv = sb("ln_mv", [P, BATCHES, 2])
        ln_ve = sb("ln_ve", [P, BATCHES])
        ln_sd = sb("ln_sd", [P, BATCHES])
        ln_rs = sb("ln_rs", [P, BATCHES])
        wq = sb("wq", [P, HEADS * HD])
        wk = sb("wk", [P, HEADS * HD])
        wv = sb("wv", [P, HEADS * HD])
        wo = sb("wo", [P, PAIRS, P])
        wf1 = sb("wf1", [P, FILT])
        wf2 = sb("wf2", [P, FILT // P, P])
        bf1c = sb("bf1c", [P, FILT // P])
        bf2b = sb("bf2b", [P, P])
        dist_g = sb("dist_g", [P, GROUP, P])
        mask_g = sb("mask_g", [P, GROUP, P])
        cst_all = sb("cst_all", [P, LAYERS, C_ALL])
        cst = sb("cst", [P, C_ALL])
        relu_z = sb("relu_z", [P, Z_SLOTS, GROUP * P])
        clamp_in = sb("clamp_in", [P, 2, GROUP * P])
        clamped = sb("clamped", [P, 2, GROUP * P])
        pool_acc = sb("pool_acc", [P, GROUP, P])
        bias_acc = sb("bias_acc", [P, GROUP * P])
        bias = sb("bias", [P, GROUP, P])
        xs = sb("xs", [P, GROUP, P])
        ctxT = sb("ctxT", [P, 2, P])
        h = sb("h", [P, 2, P])
        hT = sb("hT", [P, 2, P])
        h2 = sb("h2", [P, 2, P])
        h2T = sb("h2T", [P, 2, P])
        st = sb("st", [P, 2, 2, 6])
        mv = sb("mv", [P, 2, 2, 2])
        sd = sb("sd", [P, 2, 2])
        sde = sb("sde", [P, 2, 2])
        rs = sb("rs", [P, 2, 2])
        kT = sb("kT", [P, 2, PAIRS, P])
        qT = sb("qT", [P, 2, PAIRS, P])
        v = sb("v", [P, 2, HEADS * HD])
        score = sb("score", [P, QUADS, 4, P])
        nmax = sb("nmax", [P, QUADS, 4])
        prob = sb("prob", [P, QUADS, 4, P])
        rsum = sb("rsum", [P, QUADS, 4])
        rinv = sb("rinv", [P, QUADS, 4])
        probT = sb("probT", [P, QUADS, 4 * P])
        oT = sb("oT", [P, 2, PAIRS, P])
        hid = sb("hid", [P, 2, FILT // P, P])
        xb = sb("xb", [P, 2, P])
        gates_in = sb("gates_in", [P, 2])
        tg = sb("tg", [P, 2])
        wqk = sb("wqk", [P, 2 * P])
        wvg = sb("wvg", [P, P + EXPERTS])
        we = sb("we", [P, EXPERTS, P])
        be = sb("be", [EXPERTS, P])
        bqk = sb("bqk", [P, 2])
        bvg = sb("bvg", [P, P + EXPERTS])
        head_rows = sb("head_rows", [P, E_HEADS])
        head_mask = sb("head_mask", [P, ROW_HEADS])
        bq_mask = sb("bq_mask", [P, ROW_HEADS])
        eidx = sb("eidx", [P, EXPERTS])
        xr = sb("xr", [P, GROUP, P])
        x4 = sb("x4", [P, GROUP, P])
        delta = sb("delta", [P, 2, P])
        x1 = sb("x1", [P, GROUP, P])
        hF = sb("hF", [P, 2, P])
        hFT = sb("hFT", [P, 2, P])
        qm = sb("qm", [P, 2, ROW_HEADS, P])
        kF = sb("kF", [P, 2, P])
        vF = sb("vF", [P, 2, E_HEADS, VA])
        stF = sb("stF", [P, 2, 2, 6])
        mvF = sb("mvF", [P, 2, 2, 2])
        tinyF = sb("tinyF", [P, 2, 8])
        gate = sb("gate", [P, 2, 5, EXPERTS])
        topi = sb("topi", [P, 2, EXPERTS], U32)
        gsum = sb("gsum", [P, 2, 2])
        nmaxF = sb("nmaxF", [P, QUADS, 4])
        rinvF = sb("rinvF", [P, E_HEADS])
        comb = sb("comb", [P, 2, P])
        combT = sb("combT", [EXPERTS, 2, P])
        accF = sb("accF", [P, 2, P])
        moeF = sb("moeF", [P, P])
        attF = sb("attF", [P, P])
        oTF = sb("oTF", [P, QUADS * P])
        bothF = sb("bothF", [P, P])
        outF = sb("outF", [P, 2, P])

        def bank(name):
            return stack.enter_context(nc.psum_tensor(name, [P, 512], F32))

        L = [bank("L0"), bank("L1")]
        T = [bank("T0"), bank("T1")]
        O = bank("O")
        M0, M1, M2 = bank("M0"), bank("M1"), bank("M2")

        consts = sem("consts")
        x_in, c_in = sem("x_in"), sem("c_in")
        ln_bn, ln_mvd, ln_vd, ln_sdd, ln_rd, ln_done = [sem("ln_" + n) for n in ("bn", "mvd", "vd", "sdd", "rd", "done")]
        cT_done, cT_kept = sem("cT_done"), sem("cT_kept")
        w_k, w_v, w_q, w_o, w_f1, w_f2, w_b1, w_b2 = [sem("w_" + n) for n in "k v q o f1 f2 b1 b2".split()]
        cst_in, cst_mul, cst_ready, dist_in, cv_in, cp_in = [sem(n) for n in ("cst_in", "cst_mul", "cst_ready", "dist_in", "cv_in", "cp_in")]
        z_done, term_done, bias_done = sem("z_done"), sem("term_done"), sem("bias_done")
        pool_mul, pool_clamp, pool_sum = sem("pool_mul"), sem("pool_clamp"), sem("pool_sum")
        xs_in = [sem(f"xs_in{i}") for i in range(GROUP)]
        xs_out = [sem(f"xs_out{i}") for i in range(GROUP)]
        ctx_slot = [sem(f"ctx_slot{i}") for i in range(2)]
        bn, var, sdev, sdeps, rstd, h_done = [[sem(f"{n}{a}") for a in "ab"] for n in ("bn", "var", "sdev", "sdeps", "rstd", "h_done")]
        hT_done, hT_kept, h2T_done, h2T_kept = sem("hT_done"), sem("hT_kept"), sem("h2T_done"), sem("h2T_kept")
        k_done, v_done, q_done = sem("k_done"), sem("v_done"), sem("q_done")
        k_kept = [sem(f"k_kept{i}") for i in range(2)]
        v_kept = [sem(f"v_kept{i}") for i in range(2)]
        q_kept = [sem(f"q_kept{i}") for i in range(2)]
        qk_done, scored, exp_done, inv_done, normed = [sem(n) for n in ("qk_done", "scored", "exp_done", "inv_done", "normed")]
        pT_done = sem("pT_done")
        pT_even, pT_odd = sem("pT_even"), sem("pT_odd")
        pv_done, o_kept, wo_done = sem("pv_done"), sem("o_kept"), sem("wo_done")
        resid1, resid2, xb_done = sem("resid1"), sem("resid2"), sem("xb_done")
        f1_done, hid_kept, f2_done = sem("f1_done"), sem("hid_kept"), sem("f2_done")
        f_consts, f_in, f_gate_in, tanh_done = sem("f_consts"), sem("f_in"), sem("f_gate_in"), sem("tanh_done")
        x4_in = [sem(f"x4_in{i}") for i in range(GROUP)]
        xr_in = [sem(f"xr_in{i}") for i in range(GROUP)]
        out_st = [sem(f"out_st{i}") for i in range(2)]
        fbn, fvar, fve, fsd, fsde, frs, frg = [[sem(f"f{n}{a}") for a in "ab"] for n in ("bn", "var", "ve", "sd", "sde", "rs", "rg")]
        fdelta, fx1, fh, fhT_done, fhT_kept = [sem("f_" + n) for n in ("delta", "x1", "h", "hT_done", "hT_kept")]
        fq_done, fk_done, fv_done, fq_kept, fk_kept, fv_kept, fg_kept = [sem("f_" + n) for n in ("q_done", "k_done", "v_done", "q_kept", "k_kept", "v_kept", "g_kept")]
        fqk, fmax, fexp, fT, fT_kept, fpv, fsums, fatt = [sem("f_" + n) for n in ("qk", "max", "exp", "T", "T_kept", "pv", "sums", "att")]
        fg_top, fg_neg, fg_exp, fg_inv, fg_soft, fg_top2, fg_idx, fg_idxf, fg_c0, fg_c1, fg_comb = [sem("f_g" + n) for n in ("top", "neg", "exp", "inv", "soft", "top2", "idx", "idxf", "c0", "c1", "comb")]
        fex_acc, f_prep = [sem(f"f_ex_acc{n}") for n in range(2)], sem("f_prep")
        fcT, fcT_kept, fex, fbe, fbe_kept, fmoe, fmoe_sum, fboth, fout, fo_kept, fo_turned = [sem("f_" + n) for n in ("cT", "cT_kept", "ex", "be", "be_kept", "moe", "moe_sum", "both", "out", "o_kept", "o_turned")]

        block = stack.enter_context(nc.Block())

        def walk(eng, step, groups, first, behind, ahead=None):
            for i in range(first, GROUP):
                step(0, i)
            with eng.Fori(1, groups - 1) as g:
                for i in range(GROUP):
                    step(g, i)
            for i in range(GROUP + behind):
                if ahead and i < GROUP:
                    ahead(i)
                step(groups - 1, i)

        def walk_all(eng, step, f_step, ahead=None):
            walk(eng, step, GROUPS, -1, 0, ahead)
            f_step(0, -1)
            step(GROUPS - 1, GROUP)
            f_step(0, 0)
            step(GROUPS - 1, GROUP + 1)
            walk(eng, f_step, F_GROUPS, 1, 1)

        def there(g, i):
            return not isinstance(g, int) or 0 <= GROUP * g + i < UNITS

        def f_there(g, i):
            return not isinstance(g, int) or 0 <= GROUP * g + i < BATCHES

        def layer_of(g, i):
            return (g + i // GROUP) >> 2

        @block.sync
        def _(sp):
            def load_cst(g, a, b, signal):
                sp.dma_start(cst[:, a:b], cst_all[:, bass.ds(g >> 2, 1), a:b].rearrange("p o c -> p (o c)")).then_inc(signal, 16)

            def load_dist_rows(g):
                b = (g & 3) * GROUP
                sp.dma_start(dist_g[:, :, :], dist[bass.ds(b, GROUP), :, :].rearrange("b f t -> f b t")).then_inc(dist_in, 16)

            def load_mask(g):
                b = (g & 3) * GROUP
                sp.dma_start(mask_g[:, :, :], mask[bass.ds(b, GROUP), 0, :, :].rearrange("b o t -> o b t").broadcast_to([P, GROUP, P])).then_inc(cv_in, 16)

            def load_dist(g):
                load_dist_rows(g)
                load_cst(g, C_WTH, C_WTO, dist_in)

            def load_wto(g):
                load_cst(g, C_WTO, C_PW, cv_in)
                load_mask(g)

            def load_k(l):
                sp.dma_start(wk[:, :], Wk[bass.ds(l, 1), :, :, :].rearrange("l d n h -> d (l n h)")).then_inc(w_k, 16)

            def load_v(l):
                sp.dma_start(wv[:, :], Wv[bass.ds(l, 1), :, :, :].rearrange("l d n h -> d (l n h)")).then_inc(w_v, 16)

            def load_q(l):
                sp.dma_start(wq[:, :], Wq[bass.ds(l, 1), :, :, :].rearrange("l d n h -> d (l n h)")).then_inc(w_q, 16)

            def load_o(l):
                sp.dma_start(wo[:, :, :], Wo[bass.ds(l, 1), :, :, :].rearrange("l (j r) h d -> (r h) (l j) d", r=2)).then_inc(w_o, 16)

            def load_f1(l):
                sp.dma_start(wf1[:, :], Wf1[bass.ds(l, 1), :, :].rearrange("l d f -> d (l f)")).then_inc(w_f1, 16)

            def load_f2(l):
                sp.dma_start(wf2[:, :, :], Wf2[bass.ds(l, 1), :, :].rearrange("l (c p) d -> p (l c) d", p=P)).then_inc(w_f2, 16)

            def load_b1(l):
                sp.dma_start(bf1c[:, :], bf1[bass.ds(l, 1), :].rearrange("l (c p) -> p (l c)", p=P), allow_slow_non_contiguous=True).then_inc(w_b1, 16)

            def load_b2(l):
                sp.dma_start(bf2b[:, :], bf2[bass.ds(l, 1), :].broadcast_to([P, P])).then_inc(w_b2, 16)

            def load_x_slot(g, i):
                s = i % GROUP
                wait_first(sp, consts, xs_out[s], (g + (i // GROUP)) * 16)
                b = ((g + i // GROUP) & 3) * GROUP + s
                sp.dma_start(xs[:, s, :], x_all[:, bass.ds(b, 1), :].rearrange("p o d -> p (o d)")).then_inc(xs_in[s], 16)

            def load_ctx_slot(g, i):
                wait_first(sp, consts, v_done, after(g, i - 2, 2, 1))
                b = ((g + i // GROUP) & 3) * GROUP + i % GROUP
                sp.dma_start(ctxT[:, i % 2, :], ctxT_all[:, bass.ds(b, 1), :].rearrange("p o d -> p (o d)")).then_inc(ctx_slot[i % 2], 16)

            def store_x_slot(g, i):
                s = i % GROUP
                b = ((g + i // GROUP) & 3) * GROUP + s
                wait_first(sp, consts, resid2, after(g, i, 1))
                sp.dma_start(x_all[:, bass.ds(b, 1), :].rearrange("p o d -> p (o d)"), xs[:, s, :]).then_inc(xs_out[s], 16)

            for w, col in ((Wth.rearrange("l o k -> o l k"), C_WTH), (bth.rearrange("(o l) k -> o l k", o=1), C_BTH),
                           (Wto.rearrange("l k o -> o l k"), C_WTO)):
                sp.dma_start(cst_all[:, :, col:col + BIAS_K], w.broadcast_to([P, LAYERS, BIAS_K])).then_inc(cst_in, 16)
            sp.dma_start(cst_all[:, :, C_BTO:C_BTO + 1], bto.rearrange("(o l) k -> o l k", o=1).broadcast_to([P, LAYERS, 1]),
                         allow_slow_non_contiguous=True).then_inc(cst_in, 16)
            load_dist_rows(0)
            sp.dma_start(x_raw[:, :, :], x.rearrange("b s d -> s b d")).then_inc(x_in, 16)
            wait_first(sp, consts, cst_in, 64)
            load_cst(0, C_WTH, C_WTO, dist_in)
            load_wto(0)
            sp.dma_start(c_raw[:, :, :], ctx_in.rearrange("b t d -> t b d")).then_inc(c_in, 16)
            wait_first(sp, consts, cst_ready, 4)
            load_cst(0, C_PW, C_ALL, cp_in)
            load_k(0)
            load_v(0)
            load_q(0)
            sp.wait_ge(cT_kept, 4)
            load_ctx_slot(0, 0)
            load_ctx_slot(0, 1)
            wait_first(sp, consts, ln_done, GROUP)
            load_x_slot(0, 0)
            load_x_slot(0, 1)
            load_o(0)
            load_f1(0)
            load_f2(0)
            load_b1(0)
            load_b2(0)
            sp.dma_start(gates_in[:, 0:1], g_xattn.rearrange("(o n) -> o n", o=1).broadcast_to([P, 1])).then_inc(f_gate_in, 16)
            sp.dma_start(gates_in[:, 1:2], g_ffn.rearrange("(o n) -> o n", o=1).broadcast_to([P, 1])).then_inc(f_gate_in, 16)
            sp.dma_start(wqk[:, :], W_qkv[:, 0:2 * P]).then_inc(f_in, 16)
            sp.dma_start(wvg[:, 0:P], W_qkv[:, 2 * P:3 * P]).then_inc(f_in, 16)
            sp.dma_start(wvg[:, P:P + EXPERTS], W_gate).then_inc(f_in, 16)
            sp.dma_start(we[:, :, :], W_experts.rearrange("e d f -> d e f")).then_inc(f_in, 16)
            sp.dma_start(be[:, :], b_experts).then_inc(f_in, 16)
            sp.dma_start(bqk[:, :], b_qkv[0:2 * P].rearrange("(a p) -> p a", p=P), allow_slow_non_contiguous=True).then_inc(f_in, 16)
            sp.dma_start(bvg[:, 0:P], b_qkv[2 * P:3 * P].rearrange("(o n) -> o n", o=1).broadcast_to([P, P])).then_inc(f_in, 16)
            sp.dma_start(bvg[:, P:P + EXPERTS], b_gate.rearrange("(o n) -> o n", o=1).broadcast_to([P, EXPERTS])).then_inc(f_in, 16)
            wait_first(sp, consts, z_done, START_VEC_K)
            wait_first(sp, consts, pool_clamp, pool_count(1, 0))
            load_dist(1)
            load_cst(1, C_PW, C_ALL, cp_in)
            sp.wait_ge(bias_done, 1)
            load_wto(1)

            def group(l, gg, first=False, last=False):
                g = l * GROUPS_PER_LAYER + gg
                for i in range(GROUP):
                    if there(g, i - 2):
                        store_x_slot(g, i - 2)
                    if there(g, i + 2):
                        if first and i + 2 == GROUP:
                            wait_first(sp, consts, ln_done, BATCHES)
                        load_x_slot(g, i + 2)
                        load_ctx_slot(g, i + 2)
                    if isinstance(gg, int) and gg == 0 and not first:
                        if i == 0:
                            wait_first(sp, consts, wo_done, after(g, -1, 1))
                            load_o(l)
                            wait_first(sp, consts, xb_done, after(g, -1, 1))
                            load_b2(l)
                        if i == 1:
                            wait_first(sp, consts, f1_done, after(g, -1, 1))
                            load_f1(l)
                            wait_first(sp, consts, hid_kept, after(g, -1, 1))
                            load_b1(l)
                            wait_first(sp, consts, f2_done, after(g, -1, 1))
                            load_f2(l)
                    if isinstance(gg, int) and gg == GROUPS_PER_LAYER - 1 and not last and i == 2:
                        wait_first(sp, consts, k_done, after(g, GROUP - 1, 2, 1))
                        load_k(l + 1)
                        wait_first(sp, consts, v_done, after(g, GROUP - 1, 2, 1))
                        load_v(l + 1)
                        wait_first(sp, consts, q_done, after(g, GROUP - 1, 2, 1))
                        load_q(l + 1)
                if there(g, 2 * GROUP):
                    wait_first(sp, consts, z_done, vec_count(g + 2, 0), pool_clamp, pool_count(g + 2, 0))
                    load_dist(g + 2)
                    load_cst(g + 2, C_PW, C_ALL, cp_in)
                    wait_first(sp, consts, bias_done, g + 2)
                    load_wto(g + 2)

            def load_rows(g, i):
                s = i % GROUP
                b = (g + i // GROUP) * GROUP + s
                wait_first(sp, consts, xs_out[s], (g + i // GROUP + UNITS // GROUP - F_GROUPS + 1) * 16,
                           fx1, after(g, i - GROUP, 1))
                sp.dma_start(x4[:, s, :], x_all[:, bass.ds(b, 1), :].rearrange("p o d -> p (o d)")).then_inc(x4_in[s], 16)
                sp.dma_start(xr[:, s, :], x[bass.ds(b, 1), :, :].rearrange("o s d -> (o s) d")).then_inc(xr_in[s], 16)

            for l in range(LAYERS):
                group(l, 0, first=l == 0)
                if l == LAYERS - 1:
                    group(l, 1)
                    for i in range(3):
                        load_rows(0, i)
                    group(l, 2)
                else:
                    with sp.Fori(1, GROUPS_PER_LAYER - 1) as gg:
                        group(l, gg)
                group(l, GROUPS_PER_LAYER - 1, last=l == LAYERS - 1)
            for i in range(GROUP, GROUP + 2):
                store_x_slot(GROUPS - 1, i - 2)

            def store_rows(g, i):
                wait_first(sp, consts, fout, after(g, i, 1))
                b = (g + i // GROUP) * GROUP + i % GROUP
                sp.dma_start(out[bass.ds(b, 1), :, :].rearrange("o s d -> (o s) d"), outF[:, i % 2, :]).then_inc(out_st[i % 2], 16)

            def f_step(g, i):
                if f_there(g, i + 3):
                    load_rows(g, i + 3)
                if f_there(g, i - 1):
                    store_rows(g, i - 1)

            walk(sp, f_step, F_GROUPS, 0, 1)
            for a in range(2):
                sp.wait_ge(out_st[a], BATCHES // 2 * 16)

        @block.tensor
        def _(pe):
            mm = nc.tensor.matmul

            pe.wait_ge(consts, 3)
            pe.wait_ge(c_in, 16)
            for n in range(BATCHES // 4):
                wait(pe, cT_kept, n - 1)
                for m in range(4):
                    last = nc.tensor.transpose(T[n % 2][:, m * P:(m + 1) * P], c_raw[:, 4 * n + m, :], ident[:, :])
                last.then_inc(cT_done, 1)
            pe.wait_ge(cT_kept, 4)

            def scores(g, i, octet):
                s = i % 2
                if octet == 0:
                    for a in range(2):
                        pe.wait_ge(k_kept[a], after(g, i, 1))
                        pe.wait_ge(q_kept[a], after(g, i, 1))
                wait(pe, scored, after(g, i, 4, 2 * octet - 1))
                for m in range(4):
                    for r in range(2):
                        j = 4 * octet + m
                        last = mm(L[r][:, m * P:(m + 1) * P], qT[64 * r:64 * r + 64, s, j, :], kT[64 * r:64 * r + 64, s, j, :],
                                  start=True, stop=True)
                        if m == 3:
                            last.then_inc(qk_done, 1)

            def turn(g, i, c):
                pe.wait_ge(normed, after(g, i, 4, c))
                wait(pe, pT_odd if c % 2 else pT_even, after(g, i, 2, c // 2 - 1))
                for m in range(4):
                    last = nc.tensor.transpose(T[c % 2][:, m * P:(m + 1) * P], prob[:, c, m, :], ident[:, :])
                last.then_inc(pT_done, 1)

            def apply(g, i, octet):
                if octet == 0:
                    for a in range(2):
                        pe.wait_ge(v_kept[a], after(g, i, 1))
                pe.wait_ge(pT_even, after(g, i, 2, octet))
                pe.wait_ge(pT_odd, after(g, i, 2, octet))
                wait(pe, o_kept, after(g, i, 2, octet - 1))
                for m in range(4):
                    for r in range(2):
                        n = 8 * octet + 2 * m + r
                        last = mm(O[64 * r:64 * r + 64, m * P:(m + 1) * P], v[:, i % 2, n * HD:(n + 1) * HD],
                                  probT[:, 2 * octet + r, m * P:(m + 1) * P], start=True, stop=True)
                last.then_inc(pv_done, 1)

            def project(dst, w, src, half_):
                for m in range(4):
                    j = 4 * half_ + m
                    last = mm(dst[:, m * P:(m + 1) * P], w[:, j * P:(j + 1) * P], src, start=True, stop=True)
                return last

            def keys(g, i, a):
                if a == 0:
                    pe.wait_ge(ctx_slot[i % 2], (g * 2 + i // 2 + 1) * 16)
                    if i % GROUP == 0:
                        pe.wait_ge(w_k, layer_of(g, i) * 16 + 16)
                    wait(pe, q_kept[0], after(g, i - 1, 1))
                else:
                    pe.wait_ge(k_kept[0], after(g, i, 1))
                project(M0, wk, ctxT[:, i % 2, :], a).then_inc(k_done, 1)

            def values(g, i, a):
                if a == 0:
                    if i % GROUP == 0:
                        pe.wait_ge(w_v, layer_of(g, i) * 16 + 16)
                    wait(pe, hid_kept, after(g, i - 3, 1))
                    wait(pe, q_kept[1], after(g, i - 1, 1))
                else:
                    pe.wait_ge(k_kept[1], after(g, i, 1))
                mm((M0 if a else M1)[:, :], ctxT[:, i % 2, :], wv[:, a * 512:(a + 1) * 512], start=True, stop=True).then_inc(v_done, 1)

            def queries(g, i, a):
                if a == 0:
                    pe.wait_ge(hT_kept, after(g, i, 1))
                    if i % GROUP == 0:
                        pe.wait_ge(w_q, layer_of(g, i) * 16 + 16)
                    pe.wait_ge(v_kept[1], after(g, i, 1))
                else:
                    pe.wait_ge(v_kept[0], after(g, i, 1))
                project(M1 if a else M0, wq, hT[:, i % 2, :], a).then_inc(q_done, 1)

            def step(g, i):
                nxt, cur, prev, old = there(g, i + 1), there(g, i), there(g, i - 1), there(g, i - 2)
                if prev:
                    turn(g, i - 1, 2)
                if nxt:
                    keys(g, i + 1, 0)
                if old:
                    pe.wait_ge(h_done[1], after(g, i - 2, 1))
                    wait(pe, resid1, after(g, i - 2, 1))
                    if not prev:
                        pe.wait_ge(fbe_kept, 1)
                    elif not cur:
                        pe.wait_ge(fk_kept, 1)
                    nc.tensor.transpose(M2[:, 0:P], h2[:, i % 2, :], ident[:, :]).then_inc(h2T_done, 1)
                if cur:
                    scores(g, i, 0)
                if old:
                    pe.wait_ge(h2T_kept, after(g, i - 2, 1))
                    if i % GROUP == 2:
                        pe.wait_ge(w_f1, layer_of(g, i - 2) * 16 + 16)
                    if cur:
                        wait(pe, q_kept[1], after(g, i, 1))
                    else:
                        pe.wait_ge(hid_kept, after(g, i - 3, 1))
                        if prev:
                            pe.wait_ge(fv_kept, 1)
                            pe.wait_ge(fg_kept, 1)
                        else:
                            pe.wait_ge(fmoe, 2)
                    for c in range(FILT // P):
                        last = mm(M1[:, c * P:(c + 1) * P], wf1[:, c * P:(c + 1) * P], h2T[:, i % 2, :], start=True, stop=True)
                    last.then_inc(f1_done, 1)
                if prev:
                    turn(g, i - 1, 3)
                if nxt:
                    pe.wait_ge(h_done[0], after(g, i + 1, 1))
                    wait(pe, h2T_kept, after(g, i - 2, 1))
                    nc.tensor.transpose(M2[:, 0:P], h[:, (i + 1) % 2, :], ident[:, :]).then_inc(hT_done, 1)
                    keys(g, i + 1, 1)
                    values(g, i + 1, 0)
                if prev:
                    apply(g, i - 1, 1)
                if old:
                    pe.wait_ge(hid_kept, after(g, i - 2, 1))
                    if i % GROUP == 2:
                        pe.wait_ge(w_f2, layer_of(g, i - 2) * 16 + 16)
                    if nxt:
                        pe.wait_ge(hT_kept, after(g, i + 1, 1))
                    for c in range(FILT // P):
                        last = mm(M2[:, 0:P], hid[:, i % 2, c, :], wf2[:, c, :], start=c == 0, stop=c == FILT // P - 1)
                    last.then_inc(f2_done, 1)
                if cur:
                    turn(g, i, 0)
                    scores(g, i, 1)
                if nxt:
                    values(g, i + 1, 1)
                if prev:
                    pe.wait_ge(o_kept, after(g, i - 1, 2, 1))
                    if i % GROUP == 1:
                        pe.wait_ge(w_o, layer_of(g, i - 1) * 16 + 16)
                    if nxt:
                        pe.wait_ge(hT_kept, after(g, i + 1, 1))
                    wait(pe, resid2, after(g, i - 2, 1))
                    for j in range(PAIRS):
                        last = mm(M2[:, 0:P], oT[:, (i - 1) % 2, j, :], wo[:, j, :], start=j == 0, stop=j == PAIRS - 1)
                    last.then_inc(wo_done, 1)
                if cur:
                    turn(g, i, 1)
                if nxt:
                    queries(g, i + 1, 0)
                    queries(g, i + 1, 1)
                if cur:
                    apply(g, i, 0)


            def f_scores(g, i, c):
                if c == 0:
                    pe.wait_ge(fq_kept, after(g, i, 1))
                    pe.wait_ge(fk_kept, after(g, i, 1))
                wait(pe, fexp, after(g, i, 4, c - 2))
                rows = slice(32 * c, 32 * c + 32)
                for j in range(ROW_HEADS):
                    last = mm(L[c % 2][:, j * P:(j + 1) * P], qm[rows, i % 2, j, :], kF[rows, i % 2, :], start=True, stop=True)
                last.then_inc(fqk, 1)

            def f_turn(g, i, c):
                pe.wait_ge(fexp, after(g, i, 4, c))
                wait(pe, fT_kept, after(g, i, 4, c - 2))
                for j in range(ROW_HEADS):
                    last = nc.tensor.transpose(T[c % 2][:, j * P:(j + 1) * P], prob[:, c, j, :], ident[:, :])
                last.then_inc(fT, 1)

            def f_apply(g, i):
                pe.wait_ge(fT_kept, after(g, i, 4, 3))
                pe.wait_ge(fv_kept, after(g, i, 1))
                wait(pe, fatt, after(g, i - 1, 1))
                for c in range(QUADS):
                    for r in range(ROW_HEADS):
                        last = mm(O[VA * r:VA * r + VA, c * P:(c + 1) * P], vF[:, i % 2, ROW_HEADS * c + r, :],
                                  probT[:, c, r * P:(r + 1) * P], start=True, stop=True, tile_position=(0, VA * r))
                last.then_inc(fpv, 1)

            def f_step(g, i):
                nxt, cur, prev = f_there(g, i + 1), f_there(g, i), f_there(g, i - 1)
                if cur:
                    f_scores(g, i, 0)
                    f_scores(g, i, 1)
                if nxt:
                    pe.wait_ge(fh, after(g, i + 1, 1))
                    if isinstance(g, int) and g == 0 and i <= 0:
                        pe.wait_ge(resid1, UNITS + i)
                    elif isinstance(g, int) and g == 0 and i == 1:
                        pe.wait_ge(resid2, UNITS)
                    else:
                        pe.wait_ge(fbe_kept, after(g, i - 1, 1))
                    nc.tensor.transpose(M2[:, 0:P], hF[:, (i + 1) % 2, :], ident[:, :]).then_inc(fhT_done, 1)
                if prev:
                    f_turn(g, i - 1, 2)
                    f_turn(g, i - 1, 3)
                if nxt:
                    pe.wait_ge(fhT_kept, after(g, i + 1, 1))
                    wait(pe, fmoe, after(g, i - 1, 2, 1))
                    src = hFT[:, (i + 1) % 2, :]
                    mm(M0[:, 0:P], wqk[:, 0:P], src, start=True, stop=True).then_inc(fq_done, 1)
                    mm(M2[:, 0:P], wqk[:, P:2 * P], src, start=True, stop=True).then_inc(fk_done, 1)
                    mm(M1[:, 0:P + EXPERTS], src, wvg[:, :], start=True, stop=True).then_inc(fv_done, 1)
                if prev:
                    f_apply(g, i - 1)
                if cur:
                    f_scores(g, i, 2)
                    f_scores(g, i, 3)
                    pe.wait_ge(fg_comb, after(g, i, 1))
                    if nxt:
                        pe.wait_ge(fk_kept, after(g, i + 1, 1))
                    else:
                        pe.wait_ge(fbe_kept, after(g, i - 1, 1))
                    nc.tensor.transpose(M2[:, 0:P], comb[:, i % 2, :], ident[:, :]).then_inc(fcT, 1)
                if prev:
                    pe.wait_ge(fo_kept, after(g, i - 1, 1))
                    for c in range(QUADS):
                        last = nc.tensor.transpose(O[:, c * P:(c + 1) * P], oTF[:, c * P:(c + 1) * P], ident[:, :])
                    last.then_inc(fo_turned, 1)
                if cur:
                    f_turn(g, i, 0)
                    if nxt:
                        pe.wait_ge(fq_kept, after(g, i + 1, 1))
                        pe.wait_ge(fv_kept, after(g, i + 1, 1))
                    else:
                        pe.wait_ge(fmoe, after(g, i - 1, 2, 1))
                    for a, bank_ in enumerate((M0, M1)):
                        mm(bank_[:, :], hFT[:, i % 2, :], we[:, 4 * a:4 * a + 4, :], start=True, stop=True).then_inc(fex, 1)
                    pe.wait_ge(fcT_kept, after(g, i, 1))
                    mm(M2[:, 0:P], combT[:, i % 2, :], be[:, :], start=True, stop=True).then_inc(fbe, 1)
                    f_turn(g, i, 1)

            def ahead(i):
                if i == 0:
                    pe.wait_ge(f_in, 8 * 16)

            walk_all(pe, step, f_step, ahead)

        @block.scalar
        def _(act):
            copy = ACT.Copy
            act.wait_ge(consts, 3)
            nc.scalar.activation(tables[:, :], half[:, 0:1], ACT.Exp)
            def relu(g, k):
                if k == 0:
                    act.wait_ge(dist_in, (g + 1) * 32)
                wait(act, term_done, vec_count(g, k + 1 - Z_SLOTS))
                nc.scalar.activation(relu_z[:, z_slot(g, k), :], dist_g[:, :, :], ACT.Relu, bias=cst[:, C_BTH + k:C_BTH + k + 1],
                                     scale=cst[:, C_WTH + k:C_WTH + k + 1]).then_inc(z_done, 1)

            def relus(g, i, q):
                if i == -1:
                    for k in START_Z[q]:
                        relu(0, Z_BEFORE + k)
                elif there(g, GROUP):
                    for k in Z_PLAN[i][q] if i < GROUP else ():
                        relu(g + 1, k)

            def exps(g, i, c):
                act.wait_ge(scored, after(g, i, 4, c))
                wait(act, pT_done, after(g, i - 1, 4, c))
                wait(act, inv_done, after(g, i - 1, 4, c))
                for m in range(4):
                    last = nc.scalar.activation(prob[:, c, m, :], score[:, c, m, :], ACT.Exp, bias=nmax[:, c, m:m + 1],
                                                scale=-1.0, accum_out=rsum[:, c, m:m + 1])
                last.then_inc(exp_done, 1)

            def keep_turned(g, i, c):
                act.wait_ge(pT_done, after(g, i, 4, c))
                wait(act, pv_done, after(g, i - 1, 2, c // 2))
                nc.scalar.activation(probT[:, c, :], T[0][:, :], copy).then_inc(pT_even, 1)

            def keep_o(g, i, octet):
                act.wait_ge(pv_done, after(g, i, 2, octet))
                wait(act, wo_done, after(g, i - 2, 1))
                nc.scalar.activation(oT[:, i % 2, 4 * octet:4 * octet + 4, :], O[:, :], copy).then_inc(o_kept, 1)

            for k in range(Z_SLOTS):
                relu(0, k)
            for n in range(BATCHES // 4):
                act.wait_ge(cT_done, n + 1)
                nc.scalar.activation(ctxT_all[:, 4 * n:4 * n + 4, :], T[n % 2][:, :], copy).then_inc(cT_kept, 1)
            for k in range(Z_SLOTS, Z_BEFORE):
                relu(0, k)

            def step(g, i):
                nxt, cur, prev = there(g, i + 1), there(g, i), there(g, i - 1)
                if prev:
                    keep_turned(g, i - 1, 2)
                if nxt:
                    act.wait_ge(k_done, after(g, i + 1, 2, 0))
                    wait(act, qk_done, after(g, i - 1, 4, 3))
                    nc.scalar.activation(kT[:, (i + 1) % 2, 0:4, :], M0[:, :], copy).then_inc(k_kept[0], 1)
                relus(g, i, 0)
                if cur:
                    exps(g, i, 0)
                relus(g, i, 1)
                if nxt:
                    act.wait_ge(v_done, after(g, i + 1, 2, 0))
                    wait(act, pv_done, after(g, i - 1, 2, 1))
                    nc.scalar.activation(v[:, (i + 1) % 2, 0:512], M1[:, :], copy).then_inc(v_kept[0], 1)
                if cur:
                    exps(g, i, 1)
                if prev:
                    keep_o(g, i - 1, 1)
                if cur:
                    keep_turned(g, i, 0)
                relus(g, i, 2)
                if cur:
                    exps(g, i, 2)
                relus(g, i, 3)
                if nxt:
                    act.wait_ge(q_done, after(g, i + 1, 2, 0))
                    wait(act, qk_done, after(g, i - 1, 4, 3))
                    nc.scalar.activation(qT[:, (i + 1) % 2, 0:4, :], M0[:, :], copy, scale=HD ** -0.5).then_inc(q_kept[0], 1)
                relus(g, i, 4)
                if cur:
                    exps(g, i, 3)
                    keep_o(g, i, 0)

            def ahead(i):
                if i == 0:
                    act.wait_ge(f_gate_in, 32)
                    nc.scalar.activation(tg[:, :], gates_in[:, :], ACT.Tanh).then_inc(tanh_done, 1)
                    act.wait_ge(f_in, 8 * 16)
                if i == GROUP - 1:
                    act.wait_ge(f_consts, 6)

            def f_exps(g, i, c):
                act.wait_ge(fmax, after(g, i, 4, c))
                wait(act, fT, after(g, i - 1, 4, c))
                for j in range(4):
                    last = nc.scalar.activation(prob[:, c, j, :], L[c % 2][:, j * P:(j + 1) * P], ACT.Exp,
                                                bias=nmaxF[:, c, j:j + 1], scale=1.0)
                last.then_inc(fexp, 1)

            def f_keep(g, i, c):
                act.wait_ge(fT, after(g, i, 4, c))
                wait(act, fpv, after(g, i - 1, 1))
                nc.scalar.activation(probT[:, c, :], T[c % 2][:, :], copy).then_inc(fT_kept, 1)

            def f_step(g, i):
                nxt, cur, prev = f_there(g, i + 1), f_there(g, i), f_there(g, i - 1)
                a = (i + 1) % 2
                if nxt:
                    act.wait_ge(fhT_done, after(g, i + 1, 1))
                    wait(act, fex, after(g, i - 1, 2, 1))
                    nc.scalar.activation(hFT[:, a, :], M2[:, 0:P], copy).then_inc(fhT_kept, 1)
                if prev:
                    f_keep(g, i - 1, 2)
                    f_keep(g, i - 1, 3)
                if cur:
                    f_exps(g, i, 0)
                    f_exps(g, i, 1)
                if nxt:
                    act.wait_ge(fk_done, after(g, i + 1, 1))
                    wait(act, fqk, after(g, i - 1, 4, 3))
                    nc.scalar.activation(kF[:, a, :], M2[:, 0:P], ACT.Identity, bias=bqk[:, 1:2]).then_inc(fk_kept, 1)
                if prev:
                    act.wait_ge(fpv, after(g, i - 1, 1))
                    wait(act, fo_turned, after(g, i - 2, 1))
                    nc.scalar.activation(oTF[:, :], O[:, :], copy).then_inc(fo_kept, 1)
                if nxt:
                    act.wait_ge(fq_done, after(g, i + 1, 1))
                    for j in range(ROW_HEADS):
                        last = nc.scalar.activation(qm[:, a, j, :], M0[:, 0:P], ACT.Identity, bias=bq_mask[:, j:j + 1],
                                                    scale=head_mask[:, j:j + 1])
                    last.then_inc(fq_kept, 1)
                if cur:
                    f_exps(g, i, 2)
                if nxt:
                    act.wait_ge(fg_neg, after(g, i + 1, 1))
                    wait(act, fg_inv, after(g, i - 1, 1))
                    nc.scalar.activation(gate[:, a, 1, :], gate[:, a, 0, :], ACT.Exp, bias=gsum[:, a, 1:2], scale=1.0,
                                         accum_out=gsum[:, a, 0:1]).then_inc(fg_exp, 1)
                if cur:
                    f_exps(g, i, 3)
                    f_keep(g, i, 0)
                    f_keep(g, i, 1)

            walk_all(act, step, f_step, ahead)

        @block.vector
        def _(dve):
            vec = nc.vector
            dve.wait_ge(consts, 3)
            def cols(a):
                return cst_all[:, :, a:a + BIAS_K]

            dve.wait_ge(cst_in, 64)
            vec.tensor_tensor(cols(C_PW), cols(C_WTH), cols(C_WTO), ALU.mult).then_inc(cst_ready, 1)
            vec.tensor_tensor(cols(C_PB), cols(C_BTH), cols(C_WTO), ALU.mult).then_inc(cst_ready, 1)
            vec.tensor_scalar(cols(C_HI), cols(C_WTO), 0.0, BIG, ALU.is_ge, ALU.mult).then_inc(cst_ready, 1)
            vec.tensor_scalar(cols(C_LO), cols(C_WTO), 0.0, -BIG, ALU.is_le, ALU.mult).then_inc(cst_ready, 1)
            def term(g, k):
                if k == 0:
                    dve.wait_ge(cv_in, (g + 1) * 32)
                    wait(dve, bias_done, g)
                else:
                    dve.wait_ge(term_done, vec_count(g, k))
                dve.wait_ge(z_done, vec_count(g, k + 1))
                weight = cst[:, C_WTO + k:C_WTO + k + 1]
                if k == 0:
                    vec.tensor_scalar(bias_acc[:, :], relu_z[:, z_slot(g, k), :], weight, cst[:, C_BTO:C_BTO + 1], ALU.mult,
                                      ALU.add).then_inc(term_done, 1)
                else:
                    vec.scalar_tensor_tensor(out=bias_acc[:, :], in0=relu_z[:, z_slot(g, k), :], scalar=weight,
                                             in1=bias_acc[:, :], op0=ALU.mult, op1=ALU.add).then_inc(term_done, 1)

            for k in range(STATS_TERMS[0]):
                term(0, k)
            dve.wait_ge(x_in, 16)
            for b in range(BATCHES):
                vec.bn_stats(ln_st[:, b, :], x_raw[:, b, :]).then_inc(ln_bn, 1)
            for b in range(BATCHES):
                dve.wait_ge(ln_bn, b + 1)
                vec.bn_aggr(ln_mv[:, b, :], ln_st[:, b, :]).then_inc(ln_mvd, 1)
            dve.wait_ge(ln_mvd, BATCHES)
            vec.tensor_scalar(ln_ve[:, :], ln_mv[:, :, 1], LN_EPS, None, ALU.add).then_inc(ln_vd, 1)
            def normalise_input(batches):
                for b in batches:
                    vec.tensor_scalar(x_all[:, b, :], x_raw[:, b, :], ln_mv[:, b, 0:1], ln_rs[:, b:b + 1],
                                      ALU.subtract, ALU.mult).then_inc(ln_done, 1)

            def terms(g, i, q):
                if i == -1:
                    for k in START_TERMS[q]:
                        term(0, TERMS_BEFORE + k)
                elif there(g, GROUP):
                    for k in TERM_PLAN[i][q] if i < GROUP else ():
                        term(g + 1, k)
                elif i in EARLY_STEPS:
                    for part in F_FIRST_PARTS[q]:
                        f_first(0, EARLY_STEPS.index(i), part)

            def finish_bias(g, i):
                dve.wait_ge(pool_sum, pool_count(g + 1, 0))
                dve.wait_ge(term_done, vec_count(g + 1, 0))
                wait(dve, scored, after(g, -1, 4, 3))
                vec.tensor_tensor(bias[:, :, :], bias_acc[:, :].rearrange("p (b t) -> p b t", b=GROUP),
                                  pool_acc[:, :, :], ALU.add).then_inc(bias_done, 1)

            def score_quad(g, i, c):
                for m in range(4):
                    if m == 0:
                        if i % GROUP == 0 and c == 0:
                            dve.wait_ge(bias_done, g + i // GROUP + 1)
                        wait_first(dve, consts, qk_done, after(g, i, 4, c), exp_done, after(g, i - 1, 4, c))
                    last = vec.tensor_tensor_reduce(out=score[:, c, m, :], in0=L[c % 2][:, m * P:(m + 1) * P], in1=bias[:, i % GROUP, :],
                                                    scale=-1.0, scalar=BIG, op0=ALU.add, op1=ALU.min,
                                                    accum_out=nmax[:, c, m:m + 1])
                last.then_inc(scored, 1)

            def inverse(g, i, c):
                dve.wait_ge(exp_done, after(g, i, 4, c))
                wait(dve, normed, after(g, i - 1, 4, c))
                vec.reciprocal(rinv[:, c, :], rsum[:, c, :]).then_inc(inv_done, 1)

            def moments(g, i, a):
                s = i % 2
                if a == 0:
                    dve.wait_ge(xs_in[i % GROUP], (g + i // GROUP) * 16 + 16)
                else:
                    dve.wait_ge(resid1, after(g, i, 1))
                wait(dve, h_done[a], after(g, i - 2, 1))
                vec.bn_stats(st[:, a, s, :], xs[:, i % GROUP, :]).then_inc(bn[a], 1)
                wait_first(dve, consts, bn[a], after(g, i, 1))
                vec.bn_aggr(mv[:, a, s, :], st[:, a, s, :]).then_inc(var[a], 1)

            def scale(g, i, a):
                s = i % 2
                dve.wait_ge(sdev[a], after(g, i, 1))
                vec.tensor_scalar(sde[:, a, s:s + 1], sd[:, a, s:s + 1], NORM_EPS, None, ALU.add).then_inc(sdeps[a], 1)
                dve.wait_ge(sdeps[a], after(g, i, 1))
                vec.reciprocal(rs[:, a, s:s + 1], sde[:, a, s:s + 1]).then_inc(rstd[a], 1)

            def normalise(g, i, a):
                s = i % 2
                dve.wait_ge(rstd[a], after(g, i, 1))
                wait(dve, h2T_done if a else hT_done, after(g, i - 2, 1))
                vec.tensor_scalar((h2 if a else h)[:, s, :], xs[:, i % GROUP, :], mv[:, a, s, 0:1], rs[:, a, s:s + 1],
                                  ALU.subtract, ALU.mult).then_inc(h_done[a], 1)

            def keep_turned(g, i, c):
                dve.wait_ge(pT_done, after(g, i, 4, c))
                wait(dve, pv_done, after(g, i - 1, 2, c // 2))
                vec.tensor_copy(probT[:, c, :], T[1][:, :]).then_inc(pT_odd, 1)

            for k in range(STATS_TERMS[0], STATS_TERMS[1]):
                term(0, k)
            dve.wait_ge(ln_sdd, 1)
            vec.reciprocal(ln_rs[:, :], ln_sd[:, :]).then_inc(ln_rd, 1)
            dve.wait_ge(ln_rd, 1)
            normalise_input(range(GROUP))
            for k in range(STATS_TERMS[1], TERMS_BEFORE):
                term(0, k)
            moments(0, 0, 0)

            def step(g, i):
                nxt, cur, prev, old = there(g, i + 1), there(g, i), there(g, i - 1), there(g, i - 2)
                if prev:
                    inverse(g, i - 1, 3)
                if i < GROUP:
                    terms(g, i, 0)
                if old:
                    dve.wait_ge(h2T_done, after(g, i - 2, 1))
                    wait(dve, f1_done, after(g, i - 4, 1))
                    vec.tensor_copy(h2T[:, i % 2, :], M2[:, 0:P]).then_inc(h2T_kept, 1)
                if nxt:
                    scale(g, i + 1, 0)
                    normalise(g, i + 1, 0)
                if cur:
                    score_quad(g, i, 0)
                if old:
                    for c in range(FILT // P):
                        if c == 0:
                            dve.wait_ge(f1_done, after(g, i - 2, 1))
                            wait(dve, f2_done, after(g, i - 4, 1))
                            if i % GROUP == 2:
                                dve.wait_ge(w_b1, layer_of(g, i - 2) * 16 + 16)
                        last = vec.tensor_scalar(hid[:, i % 2, c, :], M1[:, c * P:(c + 1) * P], bf1c[:, c:c + 1], 0.0, ALU.add, ALU.max)
                    last.then_inc(hid_kept, 1)
                if prev:
                    keep_turned(g, i - 1, 3)
                if nxt:
                    dve.wait_ge(hT_done, after(g, i + 1, 1))
                    wait(dve, q_done, after(g, i - 1, 2, 1))
                    vec.tensor_copy(hT[:, (i + 1) % 2, :], M2[:, 0:P]).then_inc(hT_kept, 1)
                if isinstance(g, int) and g == 0 and i <= 0:
                    normalise_input(range(2 * GROUP, BATCHES) if i == 0 else range(GROUP, 2 * GROUP))
                if cur:
                    inverse(g, i, 0)
                    score_quad(g, i, 1)
                if nxt:
                    dve.wait_ge(k_done, after(g, i + 1, 2, 1))
                    wait(dve, qk_done, after(g, i - 1, 4, 3))
                    vec.tensor_copy(kT[:, (i + 1) % 2, 4:8, :], M0[:, :]).then_inc(k_kept[1], 1)
                terms(g, i, 1)
                if old:
                    dve.wait_ge(f2_done, after(g, i - 2, 1))
                    dve.wait_ge(xb_done, after(g, i - 2, 1))
                    vec.tensor_tensor(xs[:, (i - 2) % GROUP, :], M2[:, 0:P], xb[:, i % 2, :], ALU.add).then_inc(resid2, 1)
                if cur:
                    inverse(g, i, 1)
                terms(g, i, 2)
                if cur:
                    score_quad(g, i, 2)
                if nxt:
                    dve.wait_ge(v_done, after(g, i + 1, 2, 1))
                    wait(dve, pv_done, after(g, i - 1, 2, 1))
                    vec.tensor_copy(v[:, (i + 1) % 2, 512:1024], M0[:, :]).then_inc(v_kept[1], 1)
                if cur:
                    score_quad(g, i, 3)
                if prev:
                    dve.wait_ge(wo_done, after(g, i - 1, 1))
                    vec.tensor_tensor(xs[:, (i - 1) % GROUP, :], M2[:, 0:P], xs[:, (i - 1) % GROUP, :], ALU.add).then_inc(resid1, 1)
                if cur:
                    inverse(g, i, 2)
                    keep_turned(g, i, 1)
                if prev:
                    moments(g, i - 1, 1)
                terms(g, i, 3)
                if nxt:
                    dve.wait_ge(q_done, after(g, i + 1, 2, 1))
                    wait(dve, qk_done, after(g, i - 1, 4, 3))
                    vec.tensor_scalar(qT[:, (i + 1) % 2, 4:8, :], M1[:, :].rearrange("p (a b) -> p a b", a=4), HD ** -0.5, None,
                                      ALU.mult).then_inc(q_kept[1], 1)
                if prev:
                    scale(g, i - 1, 1)
                    normalise(g, i - 1, 1)
                if i >= 0:
                    terms(g, i, 4)
                if there(g, i + 2):
                    moments(g, i + 2, 0)
                if i == -1:
                    terms(g, i, 4)
                if i == -1:
                    finish_bias(0, 0)
                if i == GROUP - 1 and there(g, GROUP):
                    finish_bias(g + 1, 0)

            def f_first(g, i, part):
                s = i % 2
                t = tinyF[:, s, :]

                if part == 0:
                    dve.wait_ge(x4_in[i % GROUP], (g + i // GROUP) * 16 + 16)
                    wait(dve, fdelta, after(g, i - 2, 1))
                    vec.bn_stats(stF[:, 0, s, :], x4[:, i % GROUP, :]).then_inc(fbn[0], 1)
                elif part == 1:
                    wait_first(dve, consts, fbn[0], after(g, i, 1))
                    vec.bn_aggr(mvF[:, 0, s, :], stF[:, 0, s, :]).then_inc(fvar[0], 1)
                elif part == 2:
                    dve.wait_ge(fsd[0], after(g, i, 1))
                    vec.tensor_scalar(t[:, 1:2], t[:, 0:1], NORM_EPS, None, ALU.add).then_inc(fsde[0], 1)
                elif part == 3:
                    dve.wait_ge(fsde[0], after(g, i, 1))
                    vec.reciprocal(t[:, 2:3], t[:, 1:2]).then_inc(frs[0], 1)
                elif part == 4:
                    dve.wait_ge(frs[0], after(g, i, 1))
                    vec.tensor_tensor(t[:, 3:4], t[:, 2:3], tg[:, 0:1], ALU.mult).then_inc(frg[0], 1)
                elif part == 5:
                    dve.wait_ge(frg[0], after(g, i, 1))
                    wait(dve, fx1, after(g, i - 2, 1))
                    vec.tensor_scalar(delta[:, s, :], x4[:, i % GROUP, :], mvF[:, 0, s, 0:1], t[:, 3:4], ALU.subtract,
                                      ALU.mult).then_inc(fdelta, 1)
                elif part == 6:
                    dve.wait_ge(xr_in[i % GROUP], (g + i // GROUP) * 16 + 16)
                    dve.wait_ge(fdelta, after(g, i, 1))
                    wait(dve, fout, after(g, i - GROUP, 1))
                    vec.tensor_tensor(x1[:, i % GROUP, :], delta[:, s, :], xr[:, i % GROUP, :], ALU.add).then_inc(fx1, 1)
                elif part == 7:
                    dve.wait_ge(fx1, after(g, i, 1))
                    wait(dve, fh, after(g, i - 2, 1))
                    vec.bn_stats(stF[:, 1, s, :], x1[:, i % GROUP, :]).then_inc(fbn[1], 1)
                elif part == 8:
                    wait_first(dve, consts, fbn[1], after(g, i, 1))
                    vec.bn_aggr(mvF[:, 1, s, :], stF[:, 1, s, :]).then_inc(fvar[1], 1)
                elif part == 9:
                    dve.wait_ge(fvar[1], after(g, i, 1))
                    wait(dve, fsd[1], after(g, i - 2, 1))
                    vec.tensor_scalar(t[:, 4:5], mvF[:, 1, s, 1:2], LN_EPS, None, ALU.add).then_inc(fve[1], 1)
                elif part == 10:
                    dve.wait_ge(fsd[1], after(g, i, 1))
                    vec.reciprocal(t[:, 6:7], t[:, 5:6]).then_inc(frs[1], 1)
                elif part == 11:
                    dve.wait_ge(frs[1], after(g, i, 1))
                    wait(dve, fhT_done, after(g, i - 2, 1))
                    vec.tensor_scalar(hF[:, s, :], x1[:, i % GROUP, :], mvF[:, 1, s, 0:1], t[:, 6:7], ALU.subtract,
                                      ALU.mult).then_inc(fh, 1)

            def f_max(g, i, c):
                dve.wait_ge(fqk, after(g, i, 4, c))
                wait(dve, fexp, after(g, i - 1, 4, c))
                vec.tensor_reduce(nmaxF[:, c, :], L[c % 2][:, :].rearrange("p (j t) -> p j t", j=4), AX_X, ALU.max,
                                  negate=True).then_inc(fmax, 1)

            def f_gate_logits(g, i):
                s = i % 2
                dve.wait_ge(fv_done, after(g, i, 1))
                wait(dve, fg_exp, after(g, i - 2, 1))
                wait(dve, fg_c1, after(g, i - 2, 1))
                vec.tensor_tensor(gate[:, s, 0, :], M1[:, P:P + EXPERTS], bvg[:, P:P + EXPERTS], ALU.add).then_inc(fg_kept, 1)
                wait(dve, fpv, after(g, i - 2, 1))
                vec.tensor_tensor(vF[:, s, :, 0:E_HD], M1[:, 0:P].rearrange("p (n e) -> p n e", n=E_HEADS),
                                  bvg[:, 0:P].rearrange("p (n e) -> p n e", n=E_HEADS), ALU.add).then_inc(fv_kept, 1)
                wait_first(dve, consts, fg_kept, after(g, i, 1), fg_idx, after(g, i - 2, 1))
                vec.max(gate[:, s, 2, :], gate[:, s, 0, :]).then_inc(fg_top, 1)
                dve.wait_ge(fg_top, after(g, i, 1))
                wait(dve, fg_exp, after(g, i - 2, 1))
                vec.tensor_scalar(gsum[:, s, 1:2], gate[:, s, 2, 0:1], -1.0, None, ALU.mult).then_inc(fg_neg, 1)

            def f_gates(g, i, part):
                s = i % 2

                if part == 0:
                    dve.wait_ge(fg_exp, after(g, i, 1))
                    vec.reciprocal(tinyF[:, s, 7:8], gsum[:, s, 0:1]).then_inc(fg_inv, 1)
                elif part == 1:
                    dve.wait_ge(fg_inv, after(g, i, 1))
                    wait(dve, fg_idx, after(g, i - 2, 1))
                    vec.tensor_scalar(gate[:, s, 3, :], gate[:, s, 1, :], tinyF[:, s, 7:8], None, ALU.mult).then_inc(fg_soft, 1)
                elif part == 2:
                    wait_first(dve, consts, fg_neg, after(g, i, 1), fg_soft, after(g, i, 1))
                    vec.max(gate[:, s, 2, :], gate[:, s, 3, :]).then_inc(fg_top2, 1)
                elif part == 3:
                    wait_first(dve, consts, fg_top2, after(g, i, 1))
                    vec.max_index(topi[:, s, :], gate[:, s, 2, :], gate[:, s, 3, :]).then_inc(fg_idx, 1)
                elif part == 4:
                    dve.wait_ge(fg_idx, after(g, i, 1))
                    vec.tensor_copy(gate[:, s, 0, 0:2], topi[:, s, 0:2]).then_inc(fg_idxf, 1)
                elif part == 5:
                    dve.wait_ge(fg_idxf, after(g, i, 1))
                    vec.tensor_scalar(gate[:, s, 4, :], eidx[:, :], gate[:, s, 0, 0:1], gate[:, s, 2, 0:1], ALU.is_equal,
                                      ALU.mult).then_inc(fg_c0, 1)
                elif part == 6:
                    vec.tensor_scalar(gate[:, s, 1, :], eidx[:, :], gate[:, s, 0, 1:2], gate[:, s, 2, 1:2], ALU.is_equal,
                                      ALU.mult).then_inc(fg_c1, 1)
                elif part == 7:
                    dve.wait_ge(fg_c0, after(g, i, 1))
                    dve.wait_ge(fg_c1, after(g, i, 1))
                    wait(dve, fmoe, after(g, i - 2, 2, 1))
                    wait(dve, fcT, after(g, i - 2, 1))
                    vec.tensor_tensor(comb[:, s, 0:EXPERTS], gate[:, s, 4, :], gate[:, s, 1, :], ALU.add).then_inc(fg_comb, 1)

            def f_expert(g, i, e):
                s, half_, n = i % 2, e // 4, e % 4
                if n == 0:
                    dve.wait_ge(fex, after(g, i, 2, half_))
                    wait(dve, fmoe_sum, after(g, i - 1, 1))
                elif e == 5:
                    dve.wait_ge(fbe_kept, after(g, i, 1))
                else:
                    dve.wait_ge(fex_acc[half_], after(g, i, 3, n - 1))
                src, weight, acc = (M1 if half_ else M0)[:, n * P:(n + 1) * P], comb[:, s, e:e + 1], accF[:, half_, :]
                if n == 0:
                    last = vec.tensor_scalar(acc, src, weight, None, ALU.mult)
                else:
                    last = vec.scalar_tensor_tensor(out=acc, in0=src, scalar=weight, in1=acc, op0=ALU.mult, op1=ALU.add)
                last.then_inc(fex_acc[half_] if n < 3 else fmoe, 1)

            def f_expert_biases(g, i):
                dve.wait_ge(fbe, after(g, i, 1))
                dve.wait_ge(fex_acc[1], after(g, i, 3, 0))
                vec.tensor_tensor(accF[:, 1, :], M2[:, 0:P], accF[:, 1, :], ALU.add).then_inc(fbe_kept, 1)

            def f_output(g, i, part):
                s = i % 2
                o = O[:, :].rearrange("p (n e) -> p n e", e=VA)

                if part == 0:
                    dve.wait_ge(fo_turned, after(g, i, 1))
                    wait(dve, fatt, after(g, i - 1, 1))
                    vec.reciprocal(rinvF[:, :], o[:, :, E_HD]).then_inc(fsums, 1)
                elif part == 1:
                    dve.wait_ge(fsums, after(g, i, 1))
                    wait(dve, fboth, after(g, i - 1, 1))
                    vec.tensor_tensor(attF[:, :].rearrange("p (n e) -> p n e", n=E_HEADS), o[:, :, 0:E_HD],
                                      rinvF[:, :].rearrange("p (n o) -> p n o", o=1).broadcast_to([P, E_HEADS, E_HD]),
                                      ALU.mult).then_inc(fatt, 1)
                elif part == 2:
                    dve.wait_ge(fatt, after(g, i, 1))
                    dve.wait_ge(fmoe_sum, after(g, i, 1))
                    wait(dve, fout, after(g, i - 1, 1))
                    vec.tensor_tensor(bothF[:, :], attF[:, :], moeF[:, :], ALU.add).then_inc(fboth, 1)
                elif part == 3:
                    dve.wait_ge(fboth, after(g, i, 1))
                    wait(dve, out_st[s], (g * 2 + i // 2) * 16)
                    vec.scalar_tensor_tensor(out=outF[:, s, :], in0=bothF[:, :], scalar=tg[:, 1:2], in1=x1[:, i % GROUP, :],
                                             op0=ALU.mult, op1=ALU.add).then_inc(fout, 1)

            def f_step(g, i):
                far, nxt, cur, prev = i >= 0 and f_there(g, i + 2), f_there(g, i + 1), f_there(g, i), f_there(g, i - 1)

                def first(part):
                    if far:
                        f_first(g, i + 2, part)

                def gates(part):
                    if cur:
                        f_gates(g, i, part)

                def expert(e):
                    if cur:
                        f_expert(g, i, e)

                def output(part):
                    if prev:
                        f_output(g, i - 1, part)

                if cur:
                    f_max(g, i, 0)
                first(0)
                if cur:
                    f_max(g, i, 1)
                gates(0)
                first(1)
                gates(1)
                gates(2)
                first(2)
                gates(3)
                first(3)
                gates(4)
                first(4)
                gates(5)
                gates(6)
                first(5)
                gates(7)
                if nxt:
                    f_gate_logits(g, i + 1)
                if cur:
                    f_max(g, i, 2)
                first(6)
                first(7)
                first(8)
                if cur:
                    f_max(g, i, 3)
                    dve.wait_ge(fcT, after(g, i, 1))
                    wait(dve, fbe, after(g, i - 2, 1))
                    vec.tensor_copy(combT[:, i % 2, :], M2[0:EXPERTS, 0:P]).then_inc(fcT_kept, 1)
                first(9)
                expert(0)
                output(0)
                first(10)
                expert(1)
                output(1)
                expert(4)
                first(11)
                if cur:
                    f_expert_biases(g, i)
                output(2)
                expert(2)
                expert(5)
                output(3)
                expert(6)
                expert(3)
                expert(7)

            def ahead(i):
                if i == 0:
                    dve.wait_ge(tanh_done, 1)
                    dve.wait_ge(f_consts, 4)
                    dve.wait_ge(f_in, 8 * 16)
                    vec.tensor_reduce(head_mask[:, :], head_rows[:, :].rearrange("p (c j) -> p j c", j=ROW_HEADS), AX_X,
                                      ALU.add).then_inc(f_consts, 1)
                    dve.wait_ge(f_consts, 5)
                    vec.tensor_scalar(bq_mask[:, :], head_mask[:, :], bqk[:, 0:1], None, ALU.mult).then_inc(f_consts, 1)

            walk_all(dve, step, f_step, ahead)

        @block.gpsimd
        def _(pool):
            gp = nc.gpsimd
            gp.memset(half[:, :], 0.5).then_inc(consts, 1)
            gp.memset(ident[:, :], 0.0).then_inc(consts, 1)
            pool.wait_ge(consts, 2)
            gp.affine_select(out=ident[:, :], in_=ident[:, :], compare_op=ALU.not_equal, fill=1.0, base=0,
                             pattern=[[-1, P]], channel_multiplier=1).then_inc(consts, 1)

            def root(g, i, a):
                s = i % 2
                pool.wait_ge(var[a], after(g, i, 1))
                wait(pool, sdeps[a], after(g, i - 2, 1))
                gp.tensor_tensor(sd[:, a, s:s + 1], mv[:, a, s, 1:2], half[:, 0:1], ALU.pow).then_inc(sdev[a], 1)

            def norm(g, i, c):
                pool.wait_ge(inv_done, after(g, i, 4, c))
                gp.tensor_tensor(prob[:, c, :, :], prob[:, c, :, :],
                                 rinv[:, c, :].rearrange("p (m o) -> p m o", o=1).broadcast_to([P, 4, P]),
                                 ALU.mult).then_inc(normed, 1)

            def first_k(g):
                return START_POOL_SKIP if isinstance(g, int) and g == 0 else 0

            def product(g, k):
                col = VEC_K + k
                wait_first(pool, consts, *((dist_in, (g + 1) * 32, cp_in, (g + 1) * 16) if k == first_k(g) else ()),
                           pool_clamp, pool_count(g, k - 1))
                gp.tensor_scalar(clamp_in[:, k % 2, :], dist_g[:, :, :], cst[:, C_PW + col:C_PW + col + 1],
                                 cst[:, C_PB + col:C_PB + col + 1], ALU.mult, ALU.add).then_inc(pool_mul, 1)

            def clamp(g, k):
                col = VEC_K + k
                wait_first(pool, consts, pool_mul, pool_count(g, k + 1), pool_sum, pool_count(g, k - 1))
                gp.tensor_scalar(clamped[:, k % 2, :], clamp_in[:, k % 2, :], cst[:, C_HI + col:C_HI + col + 1],
                                 cst[:, C_LO + col:C_LO + col + 1], ALU.min, ALU.max).then_inc(pool_clamp, 1)

            def add(g, k):
                pool.wait_ge(pool_clamp, pool_count(g, k + 1))
                if k == first_k(g):
                    pool.wait_ge(cv_in, (g + 1) * 32)
                    wait(pool, bias_done, g)
                else:
                    pool.wait_ge(pool_sum, pool_count(g, k))
                so_far = mask_g if k == first_k(g) else pool_acc
                gp.tensor_tensor(pool_acc[:, :, :], so_far[:, :, :], clamped[:, k % 2, :].rearrange("p (b t) -> p b t", b=GROUP),
                                 ALU.add).then_inc(pool_sum, 1)

            def step(g, i):
                nxt, cur, prev = there(g, i + 1), there(g, i), there(g, i - 1)
                if nxt:
                    root(g, i + 1, 0)
                if i == -1:
                    for k in range(START_POOL_SKIP + POOL_FIRST, POOL_K):
                        product(0, k)
                        clamp(0, k)
                        add(0, k)
                if prev:
                    norm(g, i - 1, 3)
                bias_too = 0 <= i < GROUP and there(g, GROUP)
                early = i in EARLY_STEPS and not there(g, GROUP)
                if early:
                    f_root(0, EARLY_STEPS.index(i), 0)
                if bias_too:
                    product(g + 1, 2 * i)
                    clamp(g + 1, 2 * i)
                if cur:
                    norm(g, i, 0)
                if bias_too:
                    add(g + 1, 2 * i)
                    product(g + 1, 2 * i + 1)
                if cur:
                    norm(g, i, 1)
                if bias_too:
                    clamp(g + 1, 2 * i + 1)
                    add(g + 1, 2 * i + 1)
                if cur:
                    norm(g, i, 2)
                if prev:
                    root(g, i - 1, 1)
                    pool.wait_ge(resid1, after(g, i - 1, 1))
                    wait(pool, resid2, after(g, i - 3, 1))
                    if i % GROUP == 1:
                        pool.wait_ge(w_b2, layer_of(g, i - 1) * 16 + 16)
                    gp.tensor_tensor(xb[:, (i - 1) % 2, :], xs[:, (i - 1) % GROUP, :], bf2b[:, :], ALU.add).then_inc(xb_done, 1)
                if early:
                    f_root(0, EARLY_STEPS.index(i), 1)


            gp.memset(head_rows[:, :], E_HD ** -0.5).then_inc(f_prep, 1)
            gp.memset(comb[:, :, :], 0.0).then_inc(f_consts, 1)
            gp.memset(vF[:, :, :, :], 0.0).then_inc(f_prep, 1)
            gp.iota(eidx[:, :], pattern=[[1, EXPERTS]], base=0, channel_multiplier=0,
                    allow_small_or_imprecise_dtypes=True).then_inc(f_consts, 1)
            pool.wait_ge(f_prep, 2)
            gp.memset(vF[:, :, :, E_HD:E_HD + 1], 1.0).then_inc(f_consts, 1)
            gp.affine_select(out=head_rows[:, :], in_=head_rows[:, :], compare_op=ALU.is_ge, fill=0.0, base=0,
                             pattern=[[-E_HD, E_HEADS]], channel_multiplier=1).then_inc(f_prep, 1)
            pool.wait_ge(f_prep, 3)
            gp.affine_select(out=head_rows[:, :], in_=head_rows[:, :], compare_op=ALU.is_ge, fill=0.0, base=E_HD - 1,
                             pattern=[[E_HD, E_HEADS]], channel_multiplier=-1).then_inc(f_consts, 1)

            def f_root(g, i, a):
                s = i % 2
                if a == 0:
                    pool.wait_ge(fvar[0], after(g, i, 1))
                    wait(pool, fsde[0], after(g, i - 2, 1))
                    gp.tensor_tensor(tinyF[:, s, 0:1], mvF[:, 0, s, 1:2], half[:, 0:1], ALU.pow).then_inc(fsd[0], 1)
                else:
                    pool.wait_ge(fve[1], after(g, i, 1))
                    wait(pool, frs[1], after(g, i - 2, 1))
                    gp.tensor_tensor(tinyF[:, s, 5:6], tinyF[:, s, 4:5], half[:, 0:1], ALU.pow).then_inc(fsd[1], 1)

            def f_step(g, i):
                if i >= 0 and f_there(g, i + 2):
                    f_root(g, i + 2, 0)
                    f_root(g, i + 2, 1)
                if f_there(g, i):
                    pool.wait_ge(fmoe, after(g, i, 2, 1))
                    wait(pool, fboth, after(g, i - 1, 1))
                    gp.tensor_tensor(moeF[:, :], accF[:, 0, :], accF[:, 1, :], ALU.add).then_inc(fmoe_sum, 1)

            for k in range(START_POOL_SKIP, START_POOL_SKIP + POOL_FIRST):
                product(0, k)
                clamp(0, k)
                add(0, k)
                if k == START_POOL_SKIP:
                    pool.wait_ge(ln_vd, 1)
                    gp.tensor_tensor(ln_sd[:, :], ln_ve[:, :], half[:, :], ALU.pow).then_inc(ln_sdd, 1)
            walk_all(pool, step, f_step)


_INS = ["x", "ctx_1024", "fside_BxSxS2_0", "mask_Bx1x1xS2_ff0", "g_xattn", "g_ffn", "L0_xattn_Wq", "L0_xattn_Wk",
        "L0_xattn_Wv", "L0_xattn_Wo", "L0_xattn_Wth", "L0_xattn_bth", "L0_xattn_Wto", "L0_xattn_bto", "L0_xattn_Wf1",
        "L0_xattn_bf1", "L0_xattn_Wf2", "L0_xattn_bf2", "L0_ffn_W_qkv", "L0_ffn_b_qkv", "L0_ffn_W_gate", "L0_ffn_b_gate",
        "L0_ffn_W_experts", "L0_ffn_b_experts"]


def kernel(**inputs):
    import concourse.bacc as _bacc
    from concourse.bass_utils import run_bass_kernel_spmd as _run

    nc = _bacc.Bacc("TRN2", target_bir_lowering=False, num_devices=1)
    arrays, args = {}, []
    for name in _INS:
        a = np.ascontiguousarray(inputs[name])
        arrays[f"in_{name}"] = a
        args.append(nc.dram_tensor(f"in_{name}", a.shape, mybir.dt.from_np(a.dtype), kind="ExternalInput").ap())
    shape = (BATCHES, P, P)
    args.append(nc.dram_tensor("out_0", shape, F32, kind="ExternalOutput").ap())
    block_program(nc, *args)
    r = _run(nc, [arrays], core_ids=[0])
    return r.results[0]["out_0"]
```
